# Optimizing a Trainium2 kernel written in Bass

```python
import numpy as np
import jax
import jax.numpy as jnp

def _softmax(x, axis=-1):
    return jax.nn.softmax(x, axis=axis)

def _gelu(x):
    return jax.nn.gelu(x, approximate=True)

def _silu(x):
    return jax.nn.silu(x)

def _sigmoid(x):
    return jax.nn.sigmoid(x)

def _layernorm(x, axis=-1, eps=1e-05):
    m = jnp.mean(x, axis=axis, keepdims=True)
    v = jnp.var(x, axis=axis, keepdims=True)
    return (x - m) / jnp.sqrt(v + eps)

def _scatter_add(tgt, idx, src, axis=0):
    return tgt.at[idx].add(src)

def _segment_sum(src, seg, n):
    return jax.ops.segment_sum(src, seg, n)
kernel_name = 'mk_gnn_resnorm_d4_gnn_r64_02f18a'

def setup_inputs(seed: int=0):
    np.random.seed(seed)
    _w = jnp.asarray

    def _rec_inputs():
        import jax
        import jax.numpy as jnp
        _gk = jax.random.key(seed)
        x = -0.000202 + 1 * jax.random.normal(jax.random.fold_in(_gk, 1), (100000, 64), jnp.float32)
        src = jax.random.randint(jax.random.fold_in(_gk, 2), (50000,), 0, 100000, jnp.int32)
        dst = jax.random.randint(jax.random.fold_in(_gk, 3), (50000,), 0, 100000, jnp.int32)
        _o = jnp.argsort(dst, stable=True)
        src = src[_o]
        dst = dst[_o]
        edge_attr_32 = 0.000216709 + 1.00012 * jax.random.normal(jax.random.fold_in(_gk, 12), (50000, 32), jnp.float32)
        edge_attr_64 = -6.74381e-05 + 0.999835 * jax.random.normal(jax.random.fold_in(_gk, 13), (50000, 64), jnp.float32)
        edge_type_10 = jax.random.randint(jax.random.fold_in(_gk, 15), (50000,), 0, 10, jnp.int32)
        return (x, src, dst, edge_attr_32, edge_attr_64, edge_type_10)
    x, src, dst, edge_attr_32, edge_attr_64, edge_type_10 = _rec_inputs()

    def _L0_gnn_setup():
        import jax, jax.numpy as jnp
        import numpy as np
        N_NODES = 100000

        def gcn_conv(x, edge_index, W, b):
            src, dst = (edge_index[0], edge_index[1])
            n = x.shape[0]
            deg = jax.ops.segment_sum(jnp.ones(src.shape[0], dtype=x.dtype), dst, num_segments=n) + 1.0
            dinv = jax.lax.rsqrt(deg)
            h = x @ W
            coef = dinv[src] * dinv[dst]
            msg = h[src] * coef[:, None]
            agg = jax.ops.segment_sum(msg, dst, num_segments=n)
            agg = agg + h * (dinv * dinv)[:, None]
            return agg + b
        key = jax.random.key(seed)
        k0, k1, k2, k3 = jax.random.split(key, 4)
        d_in, d_hid, d_out = (64, 128, 64)
        n_edges = 25000
        x = jax.random.normal(k0, (N_NODES, d_in), dtype=jnp.float32)
        edge_index = jax.random.randint(k1, (2, n_edges), 0, N_NODES, dtype=jnp.int32)
        W1 = jax.random.normal(k2, (d_in, d_hid), dtype=jnp.float32) / np.sqrt(d_in)
        b1 = jnp.zeros((d_hid,), dtype=jnp.float32)
        W2 = jax.random.normal(k3, (d_hid, d_out), dtype=jnp.float32) / np.sqrt(d_hid)
        b2 = jnp.zeros((d_out,), dtype=jnp.float32)
        return {'x': x, 'edge_index': edge_index, 'W1': W1, 'b1': b1, 'W2': W2, 'b2': b2}
    _L0_gnn_all = _L0_gnn_setup()
    _L0_gnn_in = {k: v for k, v in _L0_gnn_all.items() if k in ('W1', 'b1', 'W2', 'b2')}
    del _L0_gnn_all

    def _L1_gnn_setup():
        import jax, jax.numpy as jnp
        import numpy as np
        N_NODES = 100000
        N_EDGES = 25000
        IN_FEAT = 64
        OUT_FEAT = 64
        key = jax.random.key(seed)
        ks = jax.random.split(key, 8)
        feature = jax.random.normal(ks[0], (N_NODES, IN_FEAT), dtype=jnp.float32)
        src = jax.random.randint(ks[1], (N_EDGES,), 0, N_NODES, dtype=jnp.int32)
        dst = jax.random.randint(ks[2], (N_EDGES,), 0, N_NODES, dtype=jnp.int32)
        W_out = jax.random.normal(ks[3], (IN_FEAT, OUT_FEAT), dtype=jnp.float32) / np.sqrt(IN_FEAT)
        b_out = jax.random.normal(ks[4], (OUT_FEAT,), dtype=jnp.float32) / np.sqrt(IN_FEAT)
        attn_w = jax.random.normal(ks[5], (2 * OUT_FEAT,), dtype=jnp.float32) / np.sqrt(2 * OUT_FEAT)
        res_W = jax.random.normal(ks[6], (IN_FEAT, OUT_FEAT), dtype=jnp.float32) / np.sqrt(IN_FEAT)
        res_b = jax.random.normal(ks[7], (OUT_FEAT,), dtype=jnp.float32) / np.sqrt(IN_FEAT)
        return {'feature': feature, 'src': src, 'dst': dst, 'W_out': W_out, 'b_out': b_out, 'attn_w': attn_w, 'res_W': res_W, 'res_b': res_b}
    _L1_gnn_all = _L1_gnn_setup()
    _L1_gnn_in = {k: v for k, v in _L1_gnn_all.items() if k in ('W_out', 'b_out', 'attn_w', 'res_W', 'res_b')}
    del _L1_gnn_all

    def _L2_gnn_setup():
        import jax, jax.numpy as jnp
        import numpy as np
        NEG_SLOPE = 0.01
        N_NODES = 100000
        N_EDGES = 1250000
        N_REL = 10
        D = 64
        key = jax.random.key(seed)
        ks = jax.random.split(key, 8)
        return {'nfeat': jax.random.normal(ks[0], (N_NODES, D), dtype=jnp.float32), 'efeat': jax.random.normal(ks[1], (N_EDGES, D), dtype=jnp.float32), 'relation_weight': jax.random.normal(ks[2], (N_REL, D, D), dtype=jnp.float32) * (1.0 / np.sqrt(D)), 'res_fc_w': jax.random.normal(ks[3], (D, D), dtype=jnp.float32) * (1.0 / np.sqrt(D)), 'res_fc2_w': jax.random.normal(ks[4], (D, D), dtype=jnp.float32) * (1.0 / np.sqrt(D)), 'src': jax.random.randint(ks[5], (N_EDGES,), 0, N_NODES, dtype=jnp.int32), 'dst': jnp.sort(jax.random.randint(ks[6], (N_EDGES,), 0, N_NODES, dtype=jnp.int32)), 'etype': jax.random.randint(ks[7], (N_EDGES,), 0, N_REL, dtype=jnp.int32)}
    _L2_gnn_all = _L2_gnn_setup()
    _L2_gnn_in = {k: v for k, v in _L2_gnn_all.items() if k in ('relation_weight', 'res_fc_w', 'res_fc2_w')}
    del _L2_gnn_all

    def _L3_gnn_setup():
        import jax, jax.numpy as jnp
        import numpy as np
        N_NODES = 50000
        N_EDGES = 12500
        D_NODE = 64
        D_EDGE = 32
        D_HID = 128

        def _mlp(x, W1, b1, W2, b2):
            return jax.nn.relu(x @ W1 + b1) @ W2 + b2
        key = jax.random.key(seed)
        ks = jax.random.split(key, 12)
        inp = {'nodes': jax.random.normal(ks[0], (N_NODES, D_NODE), dtype=jnp.float32), 'row': jax.random.randint(ks[1], (N_EDGES,), 0, N_NODES, dtype=jnp.int32), 'col': jax.random.randint(ks[2], (N_EDGES,), 0, N_NODES, dtype=jnp.int32), 'edge_features': jax.random.normal(ks[3], (N_EDGES, D_EDGE), dtype=jnp.float32)}
        d_in_msg = 2 * D_NODE + D_EDGE
        inp['mW1'] = jax.random.normal(ks[4], (d_in_msg, D_HID), dtype=jnp.float32) / np.sqrt(d_in_msg)
        inp['mb1'] = jnp.zeros((D_HID,), dtype=jnp.float32)
        inp['mW2'] = jax.random.normal(ks[5], (D_HID, D_NODE), dtype=jnp.float32) / np.sqrt(D_HID)
        inp['mb2'] = jnp.zeros((D_NODE,), dtype=jnp.float32)
        d_in_upd = 2 * D_NODE
        inp['uW1'] = jax.random.normal(ks[6], (d_in_upd, D_HID), dtype=jnp.float32) / np.sqrt(d_in_upd)
        inp['ub1'] = jnp.zeros((D_HID,), dtype=jnp.float32)
        inp['uW2'] = jax.random.normal(ks[7], (D_HID, D_NODE), dtype=jnp.float32) / np.sqrt(D_HID)
        inp['ub2'] = jnp.zeros((D_NODE,), dtype=jnp.float32)
        return inp
    _L3_gnn_all = _L3_gnn_setup()
    _L3_gnn_in = {k: v for k, v in _L3_gnn_all.items() if k in ('mW1', 'mb1', 'mW2', 'mb2', 'uW1', 'ub1', 'uW2', 'ub2')}
    del _L3_gnn_all
    return {'x': x, 'src': src, 'dst': dst, 'edge_attr_32': edge_attr_32, 'edge_attr_64': edge_attr_64, 'edge_type_10': edge_type_10, 'L0_gnn_W1': _L0_gnn_in['W1'], 'L0_gnn_b1': _L0_gnn_in['b1'], 'L0_gnn_W2': _L0_gnn_in['W2'], 'L0_gnn_b2': _L0_gnn_in['b2'], 'L1_gnn_W_out': _L1_gnn_in['W_out'], 'L1_gnn_b_out': _L1_gnn_in['b_out'], 'L1_gnn_attn_w': _L1_gnn_in['attn_w'], 'L1_gnn_res_W': _L1_gnn_in['res_W'], 'L1_gnn_res_b': _L1_gnn_in['res_b'], 'L2_gnn_relation_weight': _L2_gnn_in['relation_weight'], 'L2_gnn_res_fc_w': _L2_gnn_in['res_fc_w'], 'L2_gnn_res_fc2_w': _L2_gnn_in['res_fc2_w'], 'L3_gnn_mW1': _L3_gnn_in['mW1'], 'L3_gnn_mb1': _L3_gnn_in['mb1'], 'L3_gnn_mW2': _L3_gnn_in['mW2'], 'L3_gnn_mb2': _L3_gnn_in['mb2'], 'L3_gnn_uW1': _L3_gnn_in['uW1'], 'L3_gnn_ub1': _L3_gnn_in['ub1'], 'L3_gnn_uW2': _L3_gnn_in['uW2'], 'L3_gnn_ub2': _L3_gnn_in['ub2']}

def reference(x, src, dst, edge_attr_32, edge_attr_64, edge_type_10, L0_gnn_W1, L0_gnn_b1, L0_gnn_W2, L0_gnn_b2, L1_gnn_W_out, L1_gnn_b_out, L1_gnn_attn_w, L1_gnn_res_W, L1_gnn_res_b, L2_gnn_relation_weight, L2_gnn_res_fc_w, L2_gnn_res_fc2_w, L3_gnn_mW1, L3_gnn_mb1, L3_gnn_mW2, L3_gnn_mb2, L3_gnn_uW1, L3_gnn_ub1, L3_gnn_uW2, L3_gnn_ub2):
    import jax
    import jax.numpy as jnp

    def _L0_gnn_ref(x, edge_index, W1, b1, W2, b2):
        import jax, jax.numpy as jnp
        import numpy as np
        N_NODES = 100000

        def gcn_conv(x, edge_index, W, b):
            src, dst = (edge_index[0], edge_index[1])
            n = x.shape[0]
            deg = jax.ops.segment_sum(jnp.ones(src.shape[0], dtype=x.dtype), dst, num_segments=n) + 1.0
            dinv = jax.lax.rsqrt(deg)
            h = x @ W
            coef = dinv[src] * dinv[dst]
            msg = h[src] * coef[:, None]
            agg = jax.ops.segment_sum(msg, dst, num_segments=n)
            agg = agg + h * (dinv * dinv)[:, None]
            return agg + b
        h = gcn_conv(x, edge_index, W1, b1)
        h = jax.nn.relu(h)
        return gcn_conv(h, edge_index, W2, b2)

    def _L1_gnn_ref(feature, src, dst, W_out, b_out, attn_w, res_W, res_b):
        import jax, jax.numpy as jnp
        import numpy as np
        N_NODES = 100000
        N_EDGES = 25000
        IN_FEAT = 64
        OUT_FEAT = 64
        n = feature.shape[0]
        z = feature @ W_out + b_out
        d = z.shape[1]
        s_src = z @ attn_w[:d]
        s_dst = z @ attn_w[d:]
        e = jax.nn.gelu(s_src[src] + s_dst[dst], approximate=False)
        m = jax.ops.segment_max(e, dst, num_segments=n)
        m = jnp.where(jnp.isfinite(m), m, 0.0)
        ex = jnp.exp(e - m[dst])
        denom = jax.ops.segment_sum(ex, dst, num_segments=n)
        a = ex / jnp.maximum(denom[dst], 1e-20)
        h = jax.ops.segment_sum(a[:, None] * z[src], dst, num_segments=n)
        h = h + (feature @ res_W + res_b)
        return h

    def _L2_gnn_ref(nfeat, efeat, relation_weight, res_fc_w, res_fc2_w, src, dst, etype):
        import jax, jax.numpy as jnp
        import numpy as np
        NEG_SLOPE = 0.01
        N_NODES = 100000
        N_EDGES = 1250000
        N_REL = 10
        D = 64
        n = nfeat.shape[0]
        proj = jnp.einsum('ni,rio->nro', nfeat, relation_weight)
        t_r = proj[src, etype]
        h_r = proj[dst, etype]
        att = jnp.sum(t_r * jnp.tanh(h_r + efeat), axis=-1)
        seg_max = jax.ops.segment_max(att, dst, num_segments=n)
        ex = jnp.exp(att - seg_max[dst])
        seg_sum = jax.ops.segment_sum(ex, dst, num_segments=n)
        a = ex / seg_sum[dst]
        h_nb = jax.ops.segment_sum(nfeat[src] * a[:, None], dst, num_segments=n)
        out = jax.nn.leaky_relu((nfeat + h_nb) @ res_fc_w.T, NEG_SLOPE) + jax.nn.leaky_relu(nfeat * h_nb @ res_fc2_w.T, NEG_SLOPE)
        return out

    def _L3_gnn_ref(nodes, row, col, edge_features, mW1, mb1, mW2, mb2, uW1, ub1, uW2, ub2):
        import jax, jax.numpy as jnp
        import numpy as np
        N_NODES = 50000
        N_EDGES = 12500
        D_NODE = 64
        D_EDGE = 32
        D_HID = 128

        def _mlp(x, W1, b1, W2, b2):
            return jax.nn.relu(x @ W1 + b1) @ W2 + b2
        msg_in = jnp.concatenate([nodes[row], nodes[col], edge_features], axis=-1)
        messages = _mlp(msg_in, mW1, mb1, mW2, mb2)
        aggregated = jax.ops.segment_sum(messages, col, num_segments=nodes.shape[0])
        upd_in = jnp.concatenate([nodes, aggregated], axis=-1)
        return _mlp(upd_in, uW1, ub1, uW2, ub2)
    edge_index = jnp.stack([src, dst])
    x = _layernorm(x + _L0_gnn_ref(x, edge_index, L0_gnn_W1, L0_gnn_b1, L0_gnn_W2, L0_gnn_b2), axis=-1)
    x = _layernorm(x + _L1_gnn_ref(x, src, dst, L1_gnn_W_out, L1_gnn_b_out, L1_gnn_attn_w, L1_gnn_res_W, L1_gnn_res_b), axis=-1)
    x = _layernorm(x + _L2_gnn_ref(x, edge_attr_64, L2_gnn_relation_weight, L2_gnn_res_fc_w, L2_gnn_res_fc2_w, src, dst, edge_type_10), axis=-1)
    x = _layernorm(x + _L3_gnn_ref(x, src, dst, edge_attr_32, L3_gnn_mW1, L3_gnn_mb1, L3_gnn_mW2, L3_gnn_mb2, L3_gnn_uW1, L3_gnn_ub1, L3_gnn_uW2, L3_gnn_ub2), axis=-1)
    return x

_drawn_inputs = setup_inputs


def setup_inputs(seed=0):
    import zlib

    import numpy as np

    out = dict(_drawn_inputs(seed))
    spreads = {'L0_gnn_b1': (0.0, 0.1),
     'L0_gnn_b2': (0.0, 0.1),
     'L3_gnn_mb1': (0.0, 0.373),
     'L3_gnn_mb2': (0.0, 0.1),
     'L3_gnn_ub1': (0.0, 0.1),
     'L3_gnn_ub2': (0.0, 0.1)}
    factors = {}
    for name, (base, spread) in spreads.items():
        noise = np.random.default_rng([zlib.crc32(name.encode()), seed]).standard_normal(out[name].shape)
        drawn = base * np.exp(spread * noise) if base else spread * noise
        out[name] = jnp.asarray(drawn.astype(out[name].dtype))
    for name, factor in factors.items():
        out[name] = (out[name] * factor).astype(out[name].dtype)
    return out
```

```python
from contextlib import ExitStack

import concourse.bass as bass
from concourse import mybir

F32 = mybir.dt.float32
BF16 = mybir.dt.bfloat16
FP16 = mybir.dt.float16
I32 = mybir.dt.int32
ALU = mybir.AluOpType
ACT = mybir.ActivationFunctionType
AX_X = mybir.AxisListType.X

P = 128
NODES = 100000
EDGES = 50000
D = 64
HID = 128
DE = 32
RELS = 10
EPS = 1e-5

ROWS = 8
NODE_BLOCK = P * ROWS
NODE_BLOCKS = -(-NODES // NODE_BLOCK)
NODE_TAIL = (NODES - (NODE_BLOCKS - 1) * NODE_BLOCK) // ROWS

TILES = 4
EDGE_BLOCK = TILES * P
EDGE_BLOCKS = -(-EDGES // EDGE_BLOCK)
EDGE_TILES = -(-EDGES // P)
PAIRS = EDGE_BLOCKS // 2
assert NODE_BLOCKS == EDGE_BLOCKS == 2 * PAIRS and NODE_TAIL * ROWS == NODES % NODE_BLOCK
CHUNKS = -(-EDGE_BLOCKS * TILES // P)

NOWHERE = 200000
LOW = -1.0e30


class Signal:

    def __init__(self, ctx, nc, name):
        self.sems = [ctx.enter_context(nc.semaphore(f"{name}_{half}")) for half in range(2)]
        self.base = 0
        self.step = 1

    def __getitem__(self, half):
        return self.sems[half]

    def done(self, i):
        return i * self.step + (self.base + self.step)

    def before(self, i):
        return i * self.step + self.base

    def previous(self, i, half):
        return self.done(i) if half else self.before(i)


def later(i):
    return not (isinstance(i, int) and i == 0)


class Signals:
    def __init__(self, ctx, nc):
        self.ctx, self.nc, self.made, self.used = ctx, nc, {}, {}
        self.phase = 0

    def get(self, name, step=1):
        if name not in self.made:
            self.made[name] = Signal(self.ctx, self.nc, name)
        self.made[name].step = step
        self.used[name] = self.made[name]
        return self.made[name]

    def end_phase(self):
        for s in self.used.values():
            s.base += s.step * PAIRS
        self.used = {}
        self.phase += 1


def over_pairs(eng, body, peel_last=False):
    body(0)
    last = PAIRS - 1 if peel_last else PAIRS
    with eng.Fori(1, last) as i:
        body(i)
    if peel_last:
        body(PAIRS - 1)


def bass_gnn(nc, ins, out):
    with ExitStack() as ctx:
        build(nc, ctx, ins, out)


def build(nc, ctx, ins, out):
    sig = Signals(ctx, nc)

    def sem(name):
        return ctx.enter_context(nc.semaphore(name))

    def sb(c, name, shape, dt=F32):
        return c.enter_context(nc.sbuf_tensor(f"{name}_{sig.phase}", shape, dt))

    def pb(c, name, shape):
        return c.enter_context(nc.psum_tensor(f"{name}_{sig.phase}", shape, F32))

    def table(name):
        return nc.dram_tensor(name, (NODES, D), F32, kind="Internal").ap()

    x = ins["x"]
    y_table = table("scaled_x")
    h_table = table("scaled_h")
    x1_table = table("x_after_gcn")
    x2_table = table("x_after_attention")
    x3_table = table("x_after_relations")
    sums = table("sums_by_dst")
    same_flags = nc.dram_tensor("same_run_flags", (EDGE_BLOCKS * EDGE_BLOCK + 1,), BF16, kind="Internal").ap()

    ident = sb(ctx, "ident", [P, P])
    ones = sb(ctx, "ones", [P, P])
    src_idx = sb(ctx, "src_idx", [P, CHUNKS * P], I32)
    dst_idx = sb(ctx, "dst_idx", [P, CHUNKS * P], I32)
    dst_raw = sb(ctx, "dst_raw", [P, CHUNKS * P], I32)
    put_idx = sb(ctx, "put_idx", [P, CHUNKS * P], I32)
    dinv = sb(ctx, "dinv", [P, NODE_BLOCKS * ROWS])
    eps = sb(ctx, "eps", [P, 1])

    w1 = sb(ctx, "w1", [P, HID])
    b1 = sb(ctx, "b1", [HID, 1])
    w2 = sb(ctx, "w2", [HID, D])
    b2 = sb(ctx, "b2", [P, D])
    w_out2 = sb(ctx, "w_out2", [P, P])
    b_out2 = sb(ctx, "b_out2", [P, 1])
    attn_col = sb(ctx, "attn_col", [P, 1])
    attn_all = sb(ctx, "attn_all", [P, P])
    res_w = sb(ctx, "res_w", [P, D])
    res_b = sb(ctx, "res_b", [P, D])
    rel2 = sb(ctx, "rel2", [P, RELS, P])
    fc_raw = sb(ctx, "fc_raw", [D, 2, D])
    fc2 = sb(ctx, "fc2", [P, P])
    m_w1 = sb(ctx, "m_w1", [P, HID])
    m_w1e = sb(ctx, "m_w1e", [DE, HID])
    m_b1 = sb(ctx, "m_b1", [HID, 1])
    m_w2 = sb(ctx, "m_w2", [HID, D])
    m_b2 = sb(ctx, "m_b2", [D, 1])
    u_w1 = sb(ctx, "u_w1", [P, HID])
    u_b1 = sb(ctx, "u_b1", [HID, 1])
    u_w2 = sb(ctx, "u_w2", [HID, D])
    u_b2 = sb(ctx, "u_b2", [P, D])

    pe_passed, pool_passed, sp_passed = sem("pe_passed"), sem("pool_passed"), sem("sp_passed")
    ident_set = sem("ident_set")
    index_steps = sem("index_steps")

    def column(v):
        return v.rearrange("(d a) -> d a", a=1)

    def every_partition(v):
        return v.partition_broadcast(P)

    with ExitStack() as c:
        flat = CHUNKS * P * P
        dst_rows = sb(c, "dst_rows", [P, CHUNKS, P], I32)
        next_rows = sb(c, "next_rows", [P, CHUNKS, P], I32)
        src_rows = sb(c, "src_rows", [P, CHUNKS, P], I32)
        rows_f = sb(c, "rows_f", [P, 3, CHUNKS, P])
        same_f = sb(c, "same_f", [P, CHUNKS, P])
        same_b = sb(c, "same_b", [P, CHUNKS, P], BF16)
        zero_b = sb(c, "zero_b", [1, 1], BF16)
        zeros = sb(c, "zeros", [P, 4096])
        real = sb(c, "real", [P, CHUNKS * P])
        turned = [pb(c, f"turned{k}", [P, CHUNKS * P]) for k in range(3)]
        fc_t = pb(c, "fc_t", [D, 2, D])

        cleared = sem("cleared")
        pads_set = sem("pads_set")
        weights_in = sem("weights_in")
        rows_in = sem("rows_in")
        zeros_set = sem("zeros_set")
        prep = index_steps
        flags_made = sem("flags_made")
        flags_out = sem("flags_out")
        zeroed = sem("sums_zeroed")
        rows_turned = sem("rows_turned")
        fc_turned = sem("fc_turned")
        weights_spread = sem("weights_spread")

        WEIGHT_LOADS = 26
        full_rows = EDGES // P
        main = (CHUNKS - 1) * P
        extra = full_rows - main

        def load_rows(eng, to, vec, shift):
            n = EDGES - shift
            tail = n - full_rows * P
            eng.dma_start(to[:, 0:CHUNKS - 1, :],
                          vec[shift:shift + main * P].rearrange("(c r p) -> r c p", r=P, p=P)).then_inc(rows_in, 16)
            eng.dma_start(to[0:extra, CHUNKS - 1, :],
                          vec[shift + main * P:shift + full_rows * P].rearrange("(r p) -> r p", p=P)).then_inc(rows_in, 16)
            eng.dma_start(to[extra:extra + 1, CHUNKS - 1, 0:tail],
                          vec[shift + full_rows * P:EDGES].rearrange("(a p) -> a p", a=1)).then_inc(rows_in, 16)

        with nc.Block() as block:
            @block.gpsimd
            def _(pool):
                nc.gpsimd.memset(dst_rows[:, :, :], NOWHERE).then_inc(pads_set, 1)
                nc.gpsimd.memset(next_rows[:, :, :], -1).then_inc(pads_set, 1)
                nc.gpsimd.memset(src_rows[:, :, :], 0).then_inc(pads_set, 1)
                nc.gpsimd.memset(ident[:, :], 0.0).then_inc(ident_set, 1)
                pool.wait_ge(ident_set, 1)
                nc.gpsimd.affine_select(out=ident[:, :], in_=ident[:, :], compare_op=ALU.not_equal, fill=1.0,
                                        base=0, pattern=[[-1, P]], channel_multiplier=1).then_inc(ident_set, 1)

            @block.sync
            def _(sp):
                sp.wait_ge(pads_set, 3)
                load_rows(sp, dst_rows, ins["dst"], 0)
                load_rows(sp, next_rows, ins["dst"], 1)
                load_rows(sp, src_rows, ins["src"], 0)
                sp.wait_ge(cleared, 6)
                moves = [
                    (w1[0:D, :], ins["L0_gnn_W1"]), (w1[D:P, :], ins["L0_gnn_W1"]),
                    (b1[:, :], column(ins["L0_gnn_b1"])), (w2[:, :], ins["L0_gnn_W2"]),
                    (b2[:, :], every_partition(ins["L0_gnn_b2"])),
                    (w_out2[0:D, 0:D], ins["L1_gnn_W_out"]), (w_out2[D:P, D:P], ins["L1_gnn_W_out"]),
                    (b_out2[0:D, :], column(ins["L1_gnn_b_out"])), (b_out2[D:P, :], column(ins["L1_gnn_b_out"])),
                    (attn_col[:, :], column(ins["L1_gnn_attn_w"])),
                    (res_w[0:D, :], ins["L1_gnn_res_W"]), (res_w[D:P, :], ins["L1_gnn_res_W"]),
                    (res_b[:, :], every_partition(ins["L1_gnn_res_b"])),
                    (rel2[0:D, :, 0:D], ins["L2_gnn_relation_weight"].rearrange("r i o -> i r o")),
                    (rel2[D:P, :, D:P], ins["L2_gnn_relation_weight"].rearrange("r i o -> i r o")),
                    (fc_raw[:, 0, :], ins["L2_gnn_res_fc_w"]), (fc_raw[:, 1, :], ins["L2_gnn_res_fc2_w"]),
                    (m_w1[:, :], ins["L3_gnn_mW1"][0:P, :]), (m_w1e[:, :], ins["L3_gnn_mW1"][P:P + DE, :]),
                    (m_b1[:, :], column(ins["L3_gnn_mb1"])), (m_w2[:, :], ins["L3_gnn_mW2"]),
                    (m_b2[:, :], column(ins["L3_gnn_mb2"])),
                    (u_w1[:, :], ins["L3_gnn_uW1"]), (u_b1[:, :], column(ins["L3_gnn_ub1"])),
                    (u_w2[:, :], ins["L3_gnn_uW2"]), (u_b2[:, :], every_partition(ins["L3_gnn_ub2"])),
                ]
                assert len(moves) == WEIGHT_LOADS
                for to, of in moves:
                    sp.dma_start(to, of).then_inc(weights_in, 16)
                sp.wait_ge(flags_made, 2)
                sp.dma_start(same_flags[1:1 + main * P].rearrange("(c r p) -> r c p", r=P, p=P),
                             same_b[:, 0:CHUNKS - 1, :]).then_inc(flags_out, 16)
                left = EDGE_BLOCKS * TILES - main
                sp.dma_start(same_flags[1 + main * P:1 + (main + left) * P].rearrange("(r p) -> r p", p=P),
                             same_b[0:left, CHUNKS - 1, :]).then_inc(flags_out, 16)
                sp.dma_start(same_flags[0:1].rearrange("(a p) -> a p", a=1), zero_b[:, :]).then_inc(flags_out, 16)
                sp.wait_ge(flags_out, 48)
                sp.wait_ge(weights_in, 16 * WEIGHT_LOADS)

            @block.scalar
            def _(act):
                act.wait_ge(zeros_set, 1)
                per = 4000
                flat_sums = sums.rearrange("(p r) d -> p (r d)", p=80)
                for k in range(NODES * D // 80 // per):
                    act.dma_start(flat_sums[:, k * per:(k + 1) * per], zeros[0:80, 0:per]).then_inc(zeroed, 16)
                act.wait_ge(zeroed, 16 * (NODES * D // 80 // per))

            @block.tensor
            def _(pe):
                pe.wait_ge(ident_set, 2)
                pe.wait_ge(weights_in, 16 * WEIGHT_LOADS)
                for k in range(2):
                    last = nc.tensor.transpose(fc_t[:, k, :], fc_raw[:, k, :], ident[0:D, 0:D])
                last.then_inc(fc_turned, 1)
                pe.wait_ge(prep, 5)
                for a in range(3):
                    for k in range(CHUNKS):
                        last = nc.tensor.transpose(turned[a][:, k * P:(k + 1) * P], rows_f[:, a, k, :], ident[:, :])
                last.then_inc(rows_turned, 1)

            @block.vector
            def _(dve):
                nc.vector.memset(zeros[:, :], 0.0).then_inc(zeros_set, 1)
                nc.vector.memset(ones[:, :], 1.0).then_inc(cleared, 1)
                nc.vector.memset(w_out2[:, :], 0.0).then_inc(cleared, 1)
                nc.vector.memset(rel2[:, :, :], 0.0).then_inc(cleared, 1)
                nc.vector.memset(fc2[:, :], 0.0).then_inc(cleared, 1)
                nc.vector.memset(eps[:, :], EPS).then_inc(cleared, 1)
                nc.vector.memset(zero_b[:, :], 0.0).then_inc(cleared, 1)
                dve.wait_ge(rows_in, 16 * 9)
                nc.vector.tensor_tensor(same_f[:, :, :], dst_rows[:, :, :], next_rows[:, :, :], ALU.is_equal).then_inc(prep, 1)
                nc.vector.tensor_copy(rows_f[:, 0], src_rows[:, :, :]).then_inc(prep, 1)
                nc.vector.tensor_copy(rows_f[:, 1], dst_rows[:, :, :]).then_inc(prep, 1)
                dve.wait_ge(prep, 3)
                dve.wait_ge(cleared, 6)
                nc.vector.tensor_copy(same_b[:, :, :], same_f[:, :, :]).then_inc(flags_made, 2)
                nc.vector.scalar_tensor_tensor(out=rows_f[:, 2], in0=same_f[:, :, :], scalar=float(NOWHERE),
                                               in1=rows_f[:, 1], op0=ALU.mult, op1=ALU.add).then_inc(prep, 2)
                dve.wait_ge(fc_turned, 1)
                nc.vector.tensor_copy(fc2[0:D, 0:D], fc_t[:, 0, :]).then_inc(weights_spread, 1)
                nc.vector.tensor_copy(fc2[D:P, D:P], fc_t[:, 1, :]).then_inc(weights_spread, 1)
                nc.vector.tensor_scalar(attn_all[:, :], ones[:, :], attn_col[:, 0:1], None, ALU.mult).then_inc(weights_spread, 1)
                dve.wait_ge(rows_turned, 1)
                nc.vector.tensor_copy(src_idx[:, :], turned[0][:, :]).then_inc(prep, 1)
                nc.vector.tensor_copy(put_idx[:, :], turned[2][:, :]).then_inc(prep, 1)
                nc.vector.tensor_scalar(real[:, :], turned[1][:, :], float(NODES), None, ALU.is_lt).then_inc(prep, 1)
                nc.vector.tensor_copy(dst_raw[:, :], turned[1][:, :]).then_inc(prep, 1)
                dve.wait_ge(prep, 9)
                nc.vector.tensor_tensor(dst_idx[:, :], turned[1][:, :], real[:, :], ALU.mult).then_inc(prep, 1)

    with ExitStack() as c:
        COLS = NODE_BLOCKS * ROWS
        HALF = 512
        number = sb(c, "number", [P, COLS], I32)
        number_h = sb(c, "number_h", [P, COLS], FP16)
        hi = sb(c, "hi", [P, EDGE_TILES + 1], I32)
        lo = sb(c, "lo", [P, EDGE_TILES + 1], I32)
        mid = sb(c, "mid", [P, EDGE_TILES + 1], I32)
        col_f = sb(c, "col_f", [P, EDGE_TILES + 1])
        part_f = sb(c, "part_f", [P, EDGE_TILES + 1])
        is_part = sb(c, "is_part", [P, 2, P], FP16)
        is_col = sb(c, "is_col", [P, 2, COLS], FP16)
        root = sb(c, "root", [P, COLS])
        counts = pb(c, "counts", [P, 1024])
        numbered = sem("numbered")
        split = sem("nodes_split")
        hot = [sem("one_hot_0"), sem("one_hot_1")]
        counted = [sem("counted_0"), sem("counted_1")]
        rooted = sem("rooted")
        inverted = sem("inverted")
        LOOPS = EDGE_TILES // 2
        assert EDGE_TILES == 2 * LOOPS + 1
        with nc.Block() as block:
            @block.gpsimd
            def _(pool):
                nc.gpsimd.iota(number[:, :], [[1, COLS]], base=0, channel_multiplier=0).then_inc(numbered, 1)

            @block.vector
            def _(dve):
                T = EDGE_TILES + 1
                node = dst_raw[:, 0:T]
                nc.vector.tensor_scalar(hi[:, :], node, 10, 3, ALU.arith_shift_right, ALU.logical_shift_left).then_inc(split, 1)
                nc.vector.tensor_scalar(lo[:, :], node, 7, None, ALU.bitwise_and).then_inc(split, 1)
                dve.wait_ge(split, 2)
                nc.vector.tensor_tensor(col_f[:, :], hi[:, :], lo[:, :], ALU.add).then_inc(split, 1)
                nc.vector.tensor_scalar(mid[:, :], node, 3, 127, ALU.arith_shift_right, ALU.bitwise_and).then_inc(split, 1)
                dve.wait_ge(split, 4)
                nc.vector.tensor_copy(part_f[:, :], mid[:, :]).then_inc(split, 1)
                dve.wait_ge(numbered, 1)
                nc.vector.tensor_copy(number_h[:, :], number[:, :]).then_inc(split, 1)
                dve.wait_ge(split, 6)

                def one_hot(t, h, before):
                    if before is not None:
                        dve.wait_ge(counted[h], before)
                    nc.vector.tensor_scalar(is_part[:, h], number_h[:, 0:P], part_f[:, bass.ds(t, 1)], None,
                                            ALU.is_equal).then_inc(hot[h], 1)
                    nc.vector.tensor_scalar(is_col[:, h], number_h[:, :], col_f[:, bass.ds(t, 1)], None,
                                            ALU.is_equal).then_inc(hot[h], 1)
                one_hot(0, 0, None)
                one_hot(1, 1, None)
                one_hot(2, 0, 1)
                with dve.Fori(1, LOOPS) as i:
                    one_hot(2 * i + 1, 1, i)
                    one_hot(2 * i + 2, 0, i + 1)
                dve.wait_ge(rooted, 1)
                nc.vector.reciprocal(dinv[:, :], root[:, :]).then_inc(inverted, 1)

            @block.tensor
            def _(pe):
                def count(h, done, start, stop):
                    pe.wait_ge(hot[h], done)
                    nc.tensor.matmul(counts[:, 0:HALF], is_part[:, h], is_col[:, h, 0:HALF], start=start, stop=stop)
                    nc.tensor.matmul(counts[:, HALF:COLS], is_part[:, h], is_col[:, h, HALF:COLS],
                                     start=start, stop=stop).then_inc(counted[h], 1)
                count(0, 2, True, False)
                with pe.Fori(0, LOOPS - 1) as i:
                    count(1, 2 * i + 2, False, False)
                    count(0, 2 * i + 4, False, False)
                count(1, 2 * LOOPS, False, False)
                count(0, 2 * LOOPS + 2, False, True)

            @block.scalar
            def _(act):
                act.wait_ge(counted[0], LOOPS + 1)
                nc.scalar.activation(root[:, 0:COLS], counts[:, 0:COLS], ACT.Sqrt, bias=ones[:, 0:1]).then_inc(rooted, 1)

    def node_rows(t, i, half):
        return t[bass.ds((i * 2 + half) * NODE_BLOCK, NODE_BLOCK), :].rearrange("(p j) d -> p j d", j=ROWS)

    def tail_rows(t):
        return t[(NODE_BLOCKS - 1) * NODE_BLOCK:NODES, :].rearrange("(p j) d -> p j d", j=ROWS)

    def is_tail(i, half):
        return isinstance(i, int) and i == PAIRS - 1 and half == 1

    def move_nodes(sp, loads, stores, loaded, stored, free, ready):
        def load(i, half):
            for f in free:
                if later(i):
                    sp.wait_ge(f[half], f.before(i))
                sp.sem_inc(sp_passed, 1)
            for t, buf in loads:
                if is_tail(i, half):
                    sp.dma_start(buf(half)[0:NODE_TAIL], tail_rows(t)).then_inc(loaded[half], 16)
                else:
                    sp.dma_start(buf(half), node_rows(t, i, half)).then_inc(loaded[half], 16)

        def store(i, half):
            sp.wait_ge(ready[half], ready.done(i))
            sp.sem_inc(sp_passed, 1)
            for t, buf in stores:
                if is_tail(i, half):
                    sp.dma_start(tail_rows(t), buf(half)[0:NODE_TAIL]).then_inc(stored[half], 16)
                else:
                    sp.dma_start(node_rows(t, i, half), buf(half)).then_inc(stored[half], 16)

        def body(i):
            for half in range(2):
                load(i, half)
                if later(i):
                    store(i - 1, half)
        over_pairs(sp, body, peel_last=True)
        for half in range(2):
            store(PAIRS - 1, half)
        for half in range(2):
            sp.wait_ge(stored[half], stored.done(PAIRS - 1))

    def dinv_of(i, half):
        return dinv[:, bass.ds((i * 2 + half) * ROWS, ROWS)].unsqueeze(2).to_broadcast([P, ROWS, D])

    def over_rows(v):
        return v[:, :].unsqueeze(1).to_broadcast([P, ROWS, D])

    def of_row(v):
        return v.unsqueeze(2).to_broadcast([P, ROWS, D])

    class Norm:

        def __init__(self, c):
            self.total = sb(c, "norm_total", [P, 2, ROWS])
            self.mean = sb(c, "norm_mean", [P, 2, ROWS])
            self.centred = sb(c, "norm_centred", [P, 2, ROWS, D])
            self.square = sb(c, "norm_square", [P, 2, ROWS, D])
            self.power = sb(c, "norm_power", [P, 2, ROWS])
            self.deviation = sb(c, "norm_deviation", [P, 2, ROWS])
            self.scale = sb(c, "norm_scale", [P, 2, ROWS])
            self.out = sb(c, "norm_out", [P, 2, ROWS, D])
            self.totalled, self.averaged, self.shifted = sig.get("totalled"), sig.get("averaged"), sig.get("shifted")
            self.squared, self.powered = sig.get("squared"), sig.get("powered")
            self.rooted, self.scaled, self.ready = sig.get("deviated"), sig.get("scale_made"), sig.get("normed")

        def centre(self, dve, i, h, rows):
            nc.vector.tensor_reduce(self.total[:, h], rows, AX_X, ALU.add).then_inc(self.totalled[h], 1)
            dve.wait_ge(self.totalled[h], self.totalled.done(i))
            nc.vector.tensor_scalar(self.mean[:, h], self.total[:, h], 1.0 / D, None, ALU.mult).then_inc(self.averaged[h], 1)
            dve.wait_ge(self.averaged[h], self.averaged.done(i))
            nc.vector.tensor_tensor(self.centred[:, h], rows, of_row(self.mean[:, h]), ALU.subtract).then_inc(self.shifted[h], 1)

        def squares(self, act, i, h):
            act.wait_ge(self.shifted[h], self.shifted.done(i))
            nc.scalar.activation(self.square[:, h], self.centred[:, h], ACT.Square).then_inc(self.squared[h], 1)

        def power_of(self, dve, i, h):
            dve.wait_ge(self.squared[h], self.squared.done(i))
            nc.vector.tensor_reduce(self.power[:, h], self.square[:, h], AX_X, ALU.add).then_inc(self.powered[h], 1)

        def deviations(self, act, i, h):
            act.wait_ge(self.powered[h], self.powered.done(i))
            nc.scalar.activation(self.deviation[:, h], self.power[:, h], ACT.Sqrt, bias=eps[:, 0:1],
                                 scale=1.0 / D).then_inc(self.rooted[h], 1)

        def finish(self, dve, i, h, stored):
            dve.wait_ge(self.rooted[h], self.rooted.done(i))
            nc.vector.reciprocal(self.scale[:, h], self.deviation[:, h]).then_inc(self.scaled[h], 1)
            dve.wait_ge(self.scaled[h], self.scaled.done(i))
            if later(i):
                dve.wait_ge(stored[h], stored.before(i))
            nc.vector.tensor_tensor(self.out[:, h], self.centred[:, h], of_row(self.scale[:, h]), ALU.mult).then_inc(self.ready[h], 1)

    def scale_phase():
        with ExitStack() as c:
            xt = sb(c, "sc_x", [P, 2, ROWS, D])
            yt = sb(c, "sc_y", [P, 2, ROWS, D])
            loaded, stored = sig.get("nodes_loaded", 16), sig.get("nodes_stored", 16)
            ready = sig.get("node_result")
            with nc.Block() as block:
                @block.sync
                def _(sp):
                    move_nodes(sp, [(x, lambda h: xt[:, h])], [(y_table, lambda h: yt[:, h])],
                               loaded, stored, [ready], ready)

                @block.vector
                def _(dve):
                    def body(i):
                        for h in range(2):
                            dve.wait_ge(loaded[h], loaded.done(i))
                            if later(i):
                                dve.wait_ge(stored[h], stored.before(i))
                            nc.vector.tensor_tensor(yt[:, h], xt[:, h], dinv_of(i, h), ALU.mult).then_inc(ready[h], 1)
                    over_pairs(dve, body)
            sig.end_phase()

    def edge_block(i, half):
        return (i * 2 + half) * EDGE_BLOCK

    def load_edges(sp, i, h, loads, loaded, free):
        for f in free:
            if later(i):
                sp.wait_ge(f[h], f.before(i))
            sp.sem_inc(sp_passed, 1)
        for to, of in loads(i, h):
            sp.dma_start(to, of).then_inc(loaded[h], 16)

    def gather(pool, i, h, tables, rows, idx, loaded, free, gathered):
        pool.wait_ge(loaded[h], loaded.done(i))
        for f in free:
            if later(i):
                pool.wait_ge(f[h], f.before(i))
        pool.sem_inc(pool_passed, 1)
        for t in range(TILES):
            for k, tab in enumerate(tables):
                nc.gpsimd.indirect_dma_start(
                    out=rows[:, h, t, k * D:(k + 1) * D], out_offset=None, in_=tab,
                    in_offset=bass.IndirectOffsetOnAxis(ap=idx[:, h, k, t:t + 1], axis=0)).then_inc(gathered[h], 16)

    def scatter(pool, i, h, rows, put, staged, scattered):
        pool.wait_ge(staged[h], staged.done(i))
        pool.sem_inc(pool_passed, 1)
        for t in range(TILES):
            nc.gpsimd.indirect_dma_start(
                out=sums, out_offset=bass.IndirectOffsetOnAxis(ap=put[:, h, t:t + 1], axis=0),
                in_=rows[:, h, t, :], in_offset=None, bounds_check=NODES - 1,
                oob_is_err=False).then_inc(scattered[h], 16)

    def pool_program(pool, gather_block, scatter_block, scattered):
        def body(i):
            for h in range(2):
                gather_block(i, h)
                if later(i):
                    scatter_block(i - 1, h)
        over_pairs(pool, body)
        for h in range(2):
            scatter_block(PAIRS - 1, h)
        for h in range(2):
            pool.wait_ge(scattered[h], scattered.done(PAIRS - 1))

    def put_block(i, h):
        return put_idx[:, bass.ds((i * 2 + h) * TILES, TILES)]

    def sum_phase(source):
        with ExitStack() as c:
            rows = sb(c, "es_rows", [P, 2, TILES, D])
            idx = sb(c, "es_idx", [P, 2, 1, TILES], I32)
            same = sb(c, "es_same", [D, 2, EDGE_BLOCK], BF16)
            scan = sb(c, "es_scan", [D, 2, EDGE_BLOCK])
            back = sb(c, "es_back", [P, 2, TILES, D])
            put = sb(c, "es_put", [P, 2, TILES], I32)
            start = sb(c, "es_start", [D, 1])
            rows_t = [pb(c, f"es_rows_t{h}", [D, EDGE_BLOCK]) for h in range(2)]
            back_t = [pb(c, f"es_back_t{h}", [P, TILES, D]) for h in range(2)]
            loaded = sig.get("edges_loaded", 32)
            gathered = sig.get("gathered", 16 * TILES)
            turned = sig.get("rows_turned")
            scanned = sig.get("scanned")
            turned_back = sig.get("turned_back")
            staged = sig.get("staged", 2)
            scattered = sig.get("scattered", 16 * TILES)
            start_set = sem(f"start_set_{source.name}")
            with nc.Block() as block:
                @block.sync
                def _(sp):
                    def loads(i, h):
                        return [(idx[:, h, 0, :], src_idx[:, bass.ds((i * 2 + h) * TILES, TILES)]),
                                (same[:, h, :], same_flags[bass.ds(edge_block(i, h), EDGE_BLOCK)].partition_broadcast(D))]

                    def body(i):
                        for h in range(2):
                            load_edges(sp, i, h, loads, loaded, [gathered, scanned])
                    over_pairs(sp, body)

                @block.gpsimd
                def _(pool):
                    pool_program(pool,
                                 lambda i, h: gather(pool, i, h, [source], rows, idx, loaded, [turned], gathered),
                                 lambda i, h: scatter(pool, i, h, back, put, staged, scattered), scattered)

                @block.tensor
                def _(pe):
                    def turn(i, h):
                        pe.wait_ge(gathered[h], gathered.done(i))
                        if later(i):
                            pe.wait_ge(scanned[h], scanned.before(i))
                        pe.sem_inc(pe_passed, 1)
                        for t in range(TILES):
                            last = nc.tensor.transpose(rows_t[h][:, t * P:(t + 1) * P], rows[:, h, t, :], ident[:, :])
                        last.then_inc(turned[h], 1)

                    def turn_back(i, h):
                        pe.wait_ge(scanned[h], scanned.done(i))
                        if later(i):
                            pe.wait_ge(staged[h], staged.before(i))
                        pe.sem_inc(pe_passed, 1)
                        for t in range(TILES):
                            last = nc.tensor.transpose(back_t[h][:, t, :], scan[:, h, t * P:(t + 1) * P], ident[0:D, 0:D])
                        last.then_inc(turned_back[h], 1)

                    def body(i):
                        turn(i, 0)
                        if later(i):
                            turn_back(i - 1, 1)
                        turn(i, 1)
                        turn_back(i, 0)
                    over_pairs(pe, body)
                    turn_back(PAIRS - 1, 1)

                @block.vector
                def _(dve):
                    nc.vector.memset(start[:, :], 0.0).then_inc(start_set, 1)
                    dve.wait_ge(start_set, 1)

                    def body(i):
                        for h in range(2):
                            dve.wait_ge(turned[h], turned.done(i))
                            dve.wait_ge(loaded[h], loaded.done(i))
                            if later(i):
                                dve.wait_ge(turned_back[h], turned_back.before(i))
                            if h or later(i):
                                dve.wait_ge(scanned[1 - h], scanned.previous(i, h))
                            carry = start[:, 0:1] if not (h or later(i)) else \
                                scan[:, 1 - h, EDGE_BLOCK - 1:EDGE_BLOCK]
                            nc.vector.tensor_tensor_scan(scan[:, h, :], same[:, h, :], rows_t[h][:, :], carry,
                                                         ALU.mult, ALU.add).then_inc(scanned[h], 1)
                    over_pairs(dve, body)

                @block.scalar
                def _(act):
                    def body(i):
                        for h in range(2):
                            act.wait_ge(turned_back[h], turned_back.done(i))
                            if later(i):
                                act.wait_ge(scattered[h], scattered.before(i))
                            nc.scalar.activation(back[:, h], back_t[h][:, :, :], ACT.Copy).then_inc(staged[h], 1)
                            nc.scalar.activation(put[:, h], put_block(i, h), ACT.Copy).then_inc(staged[h], 1)
                    over_pairs(act, body)
            sig.end_phase()

    def attention_phase(source, relations):
        with ExitStack() as c:
            rows = sb(c, "ea_rows", [P, 2, TILES, P])
            idx = sb(c, "ea_idx", [P, 2, 2, TILES], I32)
            same = sb(c, "ea_same", [P, 2, EDGE_BLOCK], BF16)
            low = sb(c, "ea_low", [P, 2, EDGE_BLOCK], BF16)
            rows_s = sb(c, "ea_rows_s", [P, 2, EDGE_BLOCK])
            value = rows_s
            peak = sb(c, "ea_peak", [P, 2, EDGE_BLOCK + 1])
            fall = sb(c, "ea_fall", [P, 2, EDGE_BLOCK])
            fell = sb(c, "ea_fell", [P, 2, EDGE_BLOCK])
            below = sb(c, "ea_below", [P, 2, EDGE_BLOCK])
            decay = sb(c, "ea_decay", [P, 2, EDGE_BLOCK])
            weight = sb(c, "ea_weight", [D, 2, EDGE_BLOCK])
            terms = sb(c, "ea_terms", [P, 2, EDGE_BLOCK])
            scan = sb(c, "ea_scan", [P, 2, EDGE_BLOCK])
            guard = sb(c, "ea_guard", [P, 2, TILES])
            share = sb(c, "ea_share", [P, 2, TILES])
            back = sb(c, "ea_back", [P, 2, TILES, D])
            put = sb(c, "ea_put", [P, 2, TILES], I32)
            start = sb(c, "ea_start", [P, 2])
            rows_t = [pb(c, f"ea_rows_t{h}", [P, EDGE_BLOCK]) for h in range(2)]
            proj_t = [pb(c, f"ea_proj_t{h}", [P, EDGE_BLOCK]) for h in range(2)]
            score_t = [pb(c, f"ea_score_t{h}", [P, EDGE_BLOCK]) for h in range(2)]
            back_t = [pb(c, f"ea_back_t{h}", [P, TILES, P]) for h in range(2)]
            loaded = sig.get("edges_loaded", 16 * (6 if relations else 3))
            gathered = sig.get("gathered", 32 * TILES)
            turned, copied, projected = sig.get("rows_turned"), sig.get("rows_copied"), sig.get("projected")
            scored, lowered, peaked, peak_kept = sig.get("scored"), sig.get("lowered"), sig.get("peaked"), sig.get("peak_kept")
            falls, fallen, belows = sig.get("falls"), sig.get("fallen"), sig.get("belows")
            decayed, weighed, termed = sig.get("decayed"), sig.get("weighed", 2), sig.get("termed")
            scanned, turned_back = sig.get("scanned"), sig.get("turned_back")
            guarded, shared = sig.get("guarded"), sig.get("shared")
            staged = sig.get("staged", 2)
            scattered = sig.get("scattered", 16 * TILES)
            activated = sig.get("activated")
            start_set = sem(f"start_set_{source.name}")
            if relations:
                masked = sb(c, "ea_masked", [P, RELS, EDGE_BLOCK])
                kind = sb(c, "ea_kind", [P, 2, EDGE_BLOCK], I32)
                feats = sb(c, "ea_feats", [P, 2, TILES, P])
                bent = sb(c, "ea_bent", [D, 2, EDGE_BLOCK])
                pair = sb(c, "ea_pair", [D, 2, EDGE_BLOCK])
                masks_made, paired = sig.get("masks_made", RELS), sig.get("paired")
                load_free = [gathered, lowered, scanned, masks_made, projected]
                zeros_set = sem("feature_zeros_set")
            else:
                score_s = sb(c, "ea_score_s", [P, 2, EDGE_BLOCK])
                projected_s = sb(c, "ea_projected_s", [P, 2, EDGE_BLOCK])
                value = projected_s
                valued = sig.get("valued")
                load_free = [gathered, lowered, scanned]
            attr = ins["edge_attr_64"]
            with nc.Block() as block:
                @block.sync
                def _(sp):
                    if relations:
                        sp.wait_ge(zeros_set, 1)

                    def loads(i, h):
                        blk = bass.ds((i * 2 + h) * TILES, TILES)
                        moves = [(idx[:, h, 0, :], src_idx[:, blk]), (idx[:, h, 1, :], dst_idx[:, blk]),
                                 (same[:, h, :], same_flags[bass.ds(edge_block(i, h), EDGE_BLOCK)].partition_broadcast(P))]
                        if relations and is_tail(i, h):
                            first = (EDGE_BLOCKS - 1) * EDGE_BLOCK
                            full = (EDGES - first) // P
                            rest = EDGES - first - full * P
                            moves += [(kind[:, h, 0:EDGES - first], ins["edge_type_10"][first:EDGES].partition_broadcast(P)),
                                      (feats[:, h, 0:full, D:P],
                                       attr[first:first + full * P, :].rearrange("(t p) d -> p t d", p=P)),
                                      (feats[0:rest, h, full, D:P], attr[first + full * P:EDGES, :])]
                        elif relations:
                            whole = attr[bass.ds(edge_block(i, h), EDGE_BLOCK), :].rearrange("(t p) d -> p t d", p=P)
                            moves += [(kind[:, h, :], ins["edge_type_10"][bass.ds(edge_block(i, h), EDGE_BLOCK)].partition_broadcast(P)),
                                      (feats[:, h, 0:2, D:P], whole[:, 0:2, :]), (feats[:, h, 2:4, D:P], whole[:, 2:4, :])]
                        return moves

                    def body(i):
                        for h in range(2):
                            load_edges(sp, i, h, loads, loaded, load_free)
                    over_pairs(sp, body, peel_last=relations)

                @block.gpsimd
                def _(pool):
                    pool_program(pool,
                                 lambda i, h: gather(pool, i, h, [source, source], rows, idx, loaded, [turned], gathered),
                                 lambda i, h: scatter(pool, i, h, back, put, staged, scattered), scattered)

                @block.tensor
                def _(pe):
                    def turn(i, h):
                        pe.wait_ge(gathered[h], gathered.done(i))
                        if later(i):
                            pe.wait_ge(copied[h], copied.before(i))
                        pe.sem_inc(pe_passed, 1)
                        for t in range(TILES):
                            last = nc.tensor.transpose(rows_t[h][:, t * P:(t + 1) * P], rows[:, h, t, :], ident[:, :])
                        last.then_inc(turned[h], 1)

                    def project(i, h):
                        if relations:
                            pe.wait_ge(masks_made[h], masks_made.done(i))
                            pe.wait_ge(loaded[h], loaded.done(i))
                            if later(i):
                                pe.wait_ge(paired[h], paired.before(i))
                            for t in range(TILES):
                                nc.tensor.matmul(proj_t[h][:, t * P:(t + 1) * P], feats[:, h, t, :], ident[:, :],
                                                 start=(t == 0), stop=False, skip_group_check=True)
                            for r in range(RELS):
                                last = nc.tensor.matmul(proj_t[h][:, :], rel2[:, r, :], masked[:, r, :],
                                                        start=False, stop=(r == RELS - 1), skip_group_check=True)
                            last.then_inc(projected[h], 1)
                        else:
                            pe.wait_ge(copied[h], copied.done(i))
                            if later(i):
                                pe.wait_ge(valued[h], valued.before(i))
                            nc.tensor.matmul(proj_t[h][:, :], w_out2[:, :], rows_s[:, h, :], start=True, stop=True).then_inc(projected[h], 1)

                    def score(i, h):
                        if relations:
                            pe.wait_ge(paired[h], paired.done(i))
                            if later(i):
                                pe.wait_ge(belows[h], belows.before(i))
                            nc.tensor.matmul(score_t[h][:, :], ones[0:D, :], pair[:, h, :], start=True, stop=True).then_inc(scored[h], 1)
                        else:
                            pe.wait_ge(valued[h], valued.done(i))
                            if later(i):
                                pe.wait_ge(activated[h], activated.before(i))
                            nc.tensor.matmul(score_t[h][:, :], attn_all[:, :], projected_s[:, h, :], start=True, stop=True).then_inc(scored[h], 1)

                    def turn_back(i, h):
                        pe.wait_ge(scanned[h], scanned.done(i))
                        if later(i):
                            pe.wait_ge(staged[h], staged.before(i))
                        pe.sem_inc(pe_passed, 1)
                        for t in range(TILES):
                            last = nc.tensor.transpose(back_t[h][:, t, :], scan[:, h, t * P:(t + 1) * P], ident[:, :])
                        last.then_inc(turned_back[h], 1)

                    def body(i):
                        turn(i, 0)
                        if later(i):
                            score(i - 1, 1)
                            turn_back(i - 1, 0)
                        project(i, 0)
                        turn(i, 1)
                        score(i, 0)
                        if later(i):
                            turn_back(i - 1, 1)
                        project(i, 1)
                    over_pairs(pe, body)
                    score(PAIRS - 1, 1)
                    turn_back(PAIRS - 1, 0)
                    turn_back(PAIRS - 1, 1)

                @block.scalar
                def _(act):
                    def copy_rows(i, h):
                        act.wait_ge(turned[h], turned.done(i))
                        if relations:
                            if later(i):
                                act.wait_ge(masks_made[h], masks_made.before(i))
                                act.wait_ge(termed[h], termed.before(i))
                        else:
                            if later(i):
                                act.wait_ge(projected[h], projected.before(i))
                        nc.scalar.activation(rows_s[:, h, :], rows_t[h][:, :], ACT.Copy).then_inc(copied[h], 1)

                    def bend(i, h):
                        act.wait_ge(projected[h], projected.done(i))
                        if relations:
                            if later(i):
                                act.wait_ge(paired[h], paired.before(i))
                            nc.scalar.activation(bent[:, h, :], proj_t[h][D:P, :], ACT.Tanh).then_inc(activated[h], 1)
                        else:
                            if later(i):
                                act.wait_ge(scored[h], scored.before(i))
                                act.wait_ge(termed[h], termed.before(i))
                            nc.scalar.activation(projected_s[:, h, :], proj_t[h][:, :], ACT.Identity,
                                                 bias=b_out2[:, 0:1]).then_inc(valued[h], 1)
                            act.wait_ge(scored[h], scored.done(i))
                            if later(i):
                                act.wait_ge(belows[h], belows.before(i))
                            nc.scalar.activation(score_s[:, h, :], score_t[h][:, :], ACT.Gelu).then_inc(activated[h], 1)

                    def weigh(i, h):
                        act.wait_ge(fallen[h], fallen.done(i))
                        if later(i):
                            act.wait_ge(scanned[h], scanned.before(i))
                        nc.scalar.activation(decay[:, h, :], fell[:, h, :], ACT.Exp).then_inc(decayed[h], 1)
                        act.wait_ge(belows[h], belows.done(i))
                        if later(i):
                            act.wait_ge(termed[h], termed.before(i))
                        nc.scalar.activation(weight[:, h, :], below[0:D, h, :], ACT.Exp).then_inc(weighed[h], 1)
                        nc.scalar.activation(terms[D:P, h, :], below[D:P, h, :], ACT.Exp).then_inc(weighed[h], 1)

                    def body(i):
                        for h in range(2):
                            copy_rows(i, h)
                            if h == 1:
                                weigh(i, 0)
                            elif later(i):
                                weigh(i - 1, 1)
                            bend(i, h)
                    over_pairs(act, body)
                    weigh(PAIRS - 1, 1)

                @block.vector
                def _(dve):
                    nc.vector.memset(start[:, 0:1], LOW).then_inc(start_set, 1)
                    nc.vector.memset(start[:, 1:2], 0.0).then_inc(start_set, 1)
                    if relations:
                        nc.vector.memset(feats[:, :, :, :], 0.0).then_inc(zeros_set, 1)
                    dve.wait_ge(start_set, 2)

                    def mask(i, h):
                        dve.wait_ge(copied[h], copied.done(i))
                        dve.wait_ge(loaded[h], loaded.done(i))
                        if h or later(i):
                            dve.wait_ge(projected[1 - h], projected.previous(i, h))
                        for r in range(RELS):
                            nc.vector.scalar_tensor_tensor(out=masked[:, r, :], in0=kind[:, h, :], scalar=float(r),
                                                           in1=rows_s[:, h, :], op0=ALU.is_equal,
                                                           op1=ALU.mult).then_inc(masks_made[h], 1)

                    def pair_up(i, h):
                        dve.wait_ge(activated[h], activated.done(i))
                        if later(i):
                            dve.wait_ge(scored[h], scored.before(i))
                        nc.vector.tensor_tensor(pair[:, h, :], proj_t[h][0:D, :], bent[:, h, :], ALU.mult).then_inc(paired[h], 1)

                    def score_of(h):
                        return score_t[h][:, :] if relations else score_s[:, h, :]

                    def soften(i, h):
                        dve.wait_ge(loaded[h], loaded.done(i))
                        if later(i):
                            dve.wait_ge(peaked[h], peaked.before(i))
                            dve.wait_ge(falls[h], falls.before(i))
                        nc.vector.tensor_scalar(low[:, h, :], same[:, h, :], -1.0, -LOW, ALU.add, ALU.mult).then_inc(lowered[h], 1)
                        if later(i):
                            dve.wait_ge(fallen[h], fallen.before(i))
                            dve.wait_ge(belows[h], belows.before(i))
                        if h or later(i):
                            dve.wait_ge(peaked[1 - h], peaked.previous(i, h))
                        carried = start[:, 0:1] if not (h or later(i)) else \
                            peak[:, 1 - h, EDGE_BLOCK:EDGE_BLOCK + 1]
                        nc.vector.tensor_copy(peak[:, h, 0:1], carried).then_inc(peak_kept[h], 1)
                        dve.wait_ge(lowered[h], lowered.done(i))
                        dve.wait_ge(peak_kept[h], peak_kept.done(i))
                        dve.wait_ge((scored if relations else activated)[h], (scored if relations else activated).done(i))
                        nc.vector.tensor_tensor_scan(peak[:, h, 1:EDGE_BLOCK + 1], low[:, h, :], score_of(h),
                                                     peak[:, h, 0:1], ALU.add, ALU.max).then_inc(peaked[h], 1)
                        dve.wait_ge(peaked[h], peaked.done(i))
                        nc.vector.tensor_tensor(fall[:, h, :], peak[:, h, 0:EDGE_BLOCK], low[:, h, :], ALU.add).then_inc(falls[h], 1)
                        if later(i):
                            dve.wait_ge(weighed[h], weighed.before(i))
                        nc.vector.tensor_tensor(below[:, h, :], score_of(h), peak[:, h, 1:EDGE_BLOCK + 1], ALU.subtract).then_inc(belows[h], 1)
                        dve.wait_ge(falls[h], falls.done(i))
                        if later(i):
                            dve.wait_ge(decayed[h], decayed.before(i))
                        nc.vector.tensor_tensor(fell[:, h, :], fall[:, h, :], peak[:, h, 1:EDGE_BLOCK + 1], ALU.subtract).then_inc(fallen[h], 1)

                    def sum_up(i, h):
                        dve.wait_ge(weighed[h], weighed.done(i))
                        dve.wait_ge(decayed[h], decayed.done(i))
                        if later(i):
                            dve.wait_ge(scanned[h], scanned.before(i))
                        nc.vector.tensor_tensor(terms[0:D, h, :], weight[:, h, :], value[0:D, h, :], ALU.mult).then_inc(termed[h], 1)
                        dve.wait_ge(termed[h], termed.done(i))
                        if h or later(i):
                            dve.wait_ge(scanned[1 - h], scanned.previous(i, h))
                        if later(i):
                            dve.wait_ge(turned_back[h], turned_back.before(i))
                        carried = start[:, 1:2] if not (h or later(i)) else \
                            scan[:, 1 - h, EDGE_BLOCK - 1:EDGE_BLOCK]
                        nc.vector.tensor_tensor_scan(scan[:, h, :], decay[:, h, :], terms[:, h, :], carried,
                                                     ALU.mult, ALU.add).then_inc(scanned[h], 1)

                    def share_out(i, h):
                        dve.wait_ge(turned_back[h], turned_back.done(i))
                        if later(i):
                            dve.wait_ge(shared[h], shared.before(i))
                        nc.vector.tensor_scalar(guard[:, h, :], back_t[h][:, :, D], 1e-20, None, ALU.max).then_inc(guarded[h], 1)
                        dve.wait_ge(guarded[h], guarded.done(i))
                        if later(i):
                            dve.wait_ge(staged[h], staged.before(i))
                        nc.vector.reciprocal(share[:, h, :], guard[:, h, :]).then_inc(shared[h], 1)
                        dve.wait_ge(shared[h], shared.done(i))
                        if later(i):
                            dve.wait_ge(scattered[h], scattered.before(i))
                        nc.vector.tensor_tensor(back[:, h], back_t[h][:, :, 0:D],
                                                share[:, h, :].unsqueeze(2).to_broadcast([P, TILES, D]),
                                                ALU.mult).then_inc(staged[h], 1)
                        nc.vector.tensor_copy(put[:, h], put_block(i, h)).then_inc(staged[h], 1)

                    def body(i):
                        first = not later(i)
                        for h in range(2):
                            if relations:
                                mask(i, h)
                            if h == 1:
                                if relations:
                                    pair_up(i, 0)
                                soften(i, 0)
                                if not first:
                                    share_out(i - 1, 1)
                                sum_up(i, 0)
                            elif not first:
                                if relations:
                                    pair_up(i - 1, 1)
                                soften(i - 1, 1)
                                share_out(i - 1, 0)
                                sum_up(i - 1, 1)
                    over_pairs(dve, body)
                    if relations:
                        pair_up(PAIRS - 1, 1)
                    soften(PAIRS - 1, 1)
                    share_out(PAIRS - 1, 0)
                    sum_up(PAIRS - 1, 1)
                    share_out(PAIRS - 1, 1)
            sig.end_phase()

    def message_phase(source):
        with ExitStack() as c:
            rows = sb(c, "em_rows", [P, 2, TILES, P])
            idx = sb(c, "em_idx", [P, 2, 2, TILES], I32)
            same = sb(c, "em_same", [D, 2, EDGE_BLOCK], BF16)
            feats = sb(c, "em_feats", [P, 2, TILES, DE])
            rows_s = sb(c, "em_rows_s", [P, 2, EDGE_BLOCK])
            feats_s = sb(c, "em_feats_s", [DE, 2, EDGE_BLOCK])
            hidden = sb(c, "em_hidden", [HID, 2, EDGE_BLOCK])
            message = sb(c, "em_message", [D, 2, EDGE_BLOCK])
            scan = sb(c, "em_scan", [D, 2, EDGE_BLOCK])
            back = sb(c, "em_back", [P, 2, TILES, D])
            put = sb(c, "em_put", [P, 2, TILES], I32)
            start = sb(c, "em_start", [D, 1])
            rows_t = [pb(c, f"em_rows_t{h}", [P, EDGE_BLOCK]) for h in range(2)]
            feats_t = pb(c, "em_feats_t", [DE, EDGE_BLOCK])
            hidden_t = [pb(c, f"em_hidden_t{h}", [HID, EDGE_BLOCK]) for h in range(2)]
            message_t = pb(c, "em_message_t", [D, EDGE_BLOCK])
            back_t = [pb(c, f"em_back_t{h}", [P, TILES, D]) for h in range(2)]
            loaded = sig.get("edges_loaded", 16 * 5)
            gathered = sig.get("gathered", 32 * TILES)
            turned, copied, projected = sig.get("rows_turned"), sig.get("rows_copied", 2), sig.get("projected")
            activated, scored, valued = sig.get("activated"), sig.get("scored"), sig.get("valued")
            scanned, turned_back = sig.get("scanned"), sig.get("turned_back")
            staged = sig.get("staged", 2)
            scattered = sig.get("scattered", 16 * TILES)
            start_set = sem("start_set_messages")
            feats_set = sem("feats_set")
            attr = ins["edge_attr_32"]
            with nc.Block() as block:
                @block.sync
                def _(sp):
                    def loads(i, h):
                        blk = bass.ds((i * 2 + h) * TILES, TILES)
                        moves = [(idx[:, h, 0, :], src_idx[:, blk]), (idx[:, h, 1, :], dst_idx[:, blk]),
                                 (same[:, h, :], same_flags[bass.ds(edge_block(i, h), EDGE_BLOCK)].partition_broadcast(D))]
                        if is_tail(i, h):
                            first = (EDGE_BLOCKS - 1) * EDGE_BLOCK
                            full = (EDGES - first) // P
                            rest = EDGES - first - full * P
                            moves += [(feats[:, h, 0:full, :],
                                       attr[first:first + full * P, :].rearrange("(t p) d -> p t d", p=P)),
                                      (feats[0:rest, h, full, :], attr[first + full * P:EDGES, :])]
                        else:
                            whole = attr[bass.ds(edge_block(i, h), EDGE_BLOCK), :].rearrange("(t p) d -> p t d", p=P)
                            moves += [(feats[:, h, 0:2, :], whole[:, 0:2, :]), (feats[:, h, 2:4, :], whole[:, 2:4, :])]
                        return moves

                    def body(i):
                        for h in range(2):
                            load_edges(sp, i, h, loads, loaded, [gathered, turned, scanned])
                    over_pairs(sp, body, peel_last=True)

                @block.gpsimd
                def _(pool):
                    pool_program(pool,
                                 lambda i, h: gather(pool, i, h, [source, source], rows, idx, loaded, [turned], gathered),
                                 lambda i, h: scatter(pool, i, h, back, put, staged, scattered), scattered)

                @block.tensor
                def _(pe):
                    def turn(i, h):
                        pe.wait_ge(loaded[h], loaded.done(i))
                        if h or later(i):
                            pe.wait_ge(copied[1 - h], copied.previous(i, h))
                        pe.sem_inc(pe_passed, 1)
                        for t in range(TILES):
                            nc.tensor.transpose(feats_t[:, t * P:(t + 1) * P], feats[:, h, t, :], ident[:, :])
                        pe.wait_ge(gathered[h], gathered.done(i))
                        pe.sem_inc(pe_passed, 1)
                        for t in range(TILES):
                            last = nc.tensor.transpose(rows_t[h][:, t * P:(t + 1) * P], rows[:, h, t, :], ident[:, :])
                        last.then_inc(turned[h], 1)

                    def hide(i, h):
                        pe.wait_ge(copied[h], copied.done(i))
                        if later(i):
                            pe.wait_ge(activated[h], activated.before(i))
                        nc.tensor.matmul(hidden_t[h][:, :], m_w1[:, :], rows_s[:, h, :], start=True, stop=False)
                        nc.tensor.matmul(hidden_t[h][:, :], m_w1e[:, :], feats_s[:, h, :], start=False,
                                         stop=True).then_inc(projected[h], 1)

                    def write(i, h):
                        pe.wait_ge(activated[h], activated.done(i))
                        if h or later(i):
                            pe.wait_ge(valued[1 - h], valued.previous(i, h))
                        nc.tensor.matmul(message_t[:, :], m_w2[:, :], hidden[:, h, :], start=True, stop=True).then_inc(scored[h], 1)

                    def turn_back(i, h):
                        pe.wait_ge(scanned[h], scanned.done(i))
                        if later(i):
                            pe.wait_ge(staged[h], staged.before(i))
                        pe.sem_inc(pe_passed, 1)
                        for t in range(TILES):
                            last = nc.tensor.transpose(back_t[h][:, t, :], scan[:, h, t * P:(t + 1) * P], ident[0:D, 0:D])
                        last.then_inc(turned_back[h], 1)

                    def body(i):
                        turn(i, 0)
                        if later(i):
                            write(i - 1, 1)
                            turn_back(i - 1, 0)
                        hide(i, 0)
                        turn(i, 1)
                        write(i, 0)
                        if later(i):
                            turn_back(i - 1, 1)
                        hide(i, 1)
                    over_pairs(pe, body)
                    write(PAIRS - 1, 1)
                    turn_back(PAIRS - 1, 0)
                    turn_back(PAIRS - 1, 1)

                @block.scalar
                def _(act):
                    def copy_rows(i, h):
                        act.wait_ge(turned[h], turned.done(i))
                        if later(i):
                            act.wait_ge(projected[h], projected.before(i))
                        nc.scalar.activation(rows_s[:, h, :], rows_t[h][:, :], ACT.Copy).then_inc(copied[h], 1)
                        nc.scalar.activation(feats_s[:, h, :], feats_t[:, :], ACT.Copy).then_inc(copied[h], 1)

                    def rectify(i, h):
                        act.wait_ge(projected[h], projected.done(i))
                        if later(i):
                            act.wait_ge(scored[h], scored.before(i))
                        nc.scalar.activation(hidden[:, h, :], hidden_t[h][:, :], ACT.Relu, bias=m_b1[:, 0:1]).then_inc(activated[h], 1)

                    def add_bias(i, h):
                        act.wait_ge(scored[h], scored.done(i))
                        if later(i):
                            act.wait_ge(scanned[h], scanned.before(i))
                        nc.scalar.activation(message[:, h, :], message_t[:, :], ACT.Identity, bias=m_b2[:, 0:1]).then_inc(valued[h], 1)

                    def body(i):
                        copy_rows(i, 0)
                        if later(i):
                            add_bias(i - 1, 1)
                        rectify(i, 0)
                        copy_rows(i, 1)
                        add_bias(i, 0)
                        rectify(i, 1)
                    over_pairs(act, body)
                    add_bias(PAIRS - 1, 1)

                @block.vector
                def _(dve):
                    nc.vector.memset(start[:, :], 0.0).then_inc(start_set, 1)
                    dve.wait_ge(start_set, 1)

                    def sum_up(i, h):
                        dve.wait_ge(valued[h], valued.done(i))
                        dve.wait_ge(loaded[h], loaded.done(i))
                        if later(i):
                            dve.wait_ge(turned_back[h], turned_back.before(i))
                        if h or later(i):
                            dve.wait_ge(scanned[1 - h], scanned.previous(i, h))
                        carried = start[:, 0:1] if not (h or later(i)) else \
                            scan[:, 1 - h, EDGE_BLOCK - 1:EDGE_BLOCK]
                        nc.vector.tensor_tensor_scan(scan[:, h, :], same[:, h, :], message[:, h, :], carried,
                                                     ALU.mult, ALU.add).then_inc(scanned[h], 1)

                    def stage(i, h):
                        dve.wait_ge(turned_back[h], turned_back.done(i))
                        if later(i):
                            dve.wait_ge(scattered[h], scattered.before(i))
                        nc.vector.tensor_copy(back[:, h], back_t[h][:, :, :]).then_inc(staged[h], 1)
                        nc.vector.tensor_copy(put[:, h], put_block(i, h)).then_inc(staged[h], 1)

                    def body(i):
                        first = not later(i)
                        if not first:
                            stage(i - 1, 0)
                            sum_up(i - 1, 1)
                            stage(i - 1, 1)
                        sum_up(i, 0)
                    over_pairs(dve, body)
                    stage(PAIRS - 1, 0)
                    sum_up(PAIRS - 1, 1)
                    stage(PAIRS - 1, 1)
            sig.end_phase()

    def gcn_phase():
        with ExitStack() as c:
            agg = sb(c, "ng_agg", [P, 2, ROWS, D])
            own = sb(c, "ng_own", [P, 2, ROWS, D])
            both = sb(c, "ng_both", [P, 2, ROWS, D])
            unit = sb(c, "ng_unit", [P, 2, ROWS, D])
            unit_s = sb(c, "ng_unit_s", [P, 2, 512])
            hidden = sb(c, "ng_hidden", [HID, 2, 2, 512])
            res = sb(c, "ng_res", [P, 2, ROWS, D])
            unit_t = [pb(c, f"ng_unit_t{h}", [P, 512]) for h in range(2)]
            hidden_t = [pb(c, f"ng_hidden_t{h}", [HID, 2, 512]) for h in range(2)]
            out_t = [pb(c, f"ng_out_t{h}", [P, ROWS, D]) for h in range(2)]
            loaded, stored = sig.get("nodes_loaded", 32), sig.get("nodes_stored", 16)
            added, united = sig.get("node_added"), sig.get("node_united")
            turned, copied = sig.get("rows_turned"), sig.get("rows_copied")
            projected, activated, scored = sig.get("projected"), sig.get("activated"), sig.get("scored")
            ready = sig.get("node_result")
            with nc.Block() as block:
                @block.sync
                def _(sp):
                    move_nodes(sp, [(sums, lambda h: agg[:, h]), (y_table, lambda h: own[:, h])],
                               [(h_table, lambda h: res[:, h])], loaded, stored, [added], ready)

                @block.vector
                def _(dve):
                    def unite(i, h):
                        dve.wait_ge(loaded[h], loaded.done(i))
                        if later(i):
                            dve.wait_ge(united[h], united.before(i))
                        nc.vector.tensor_tensor(both[:, h], agg[:, h], own[:, h], ALU.add).then_inc(added[h], 1)
                        dve.wait_ge(added[h], added.done(i))
                        if later(i):
                            dve.wait_ge(turned[h], turned.before(i))
                        nc.vector.tensor_tensor(unit[:, h], both[:, h], dinv_of(i, h), ALU.mult).then_inc(united[h], 1)

                    def finish(i, h):
                        dve.wait_ge(scored[h], scored.done(i))
                        if later(i):
                            dve.wait_ge(stored[h], stored.before(i))
                        nc.vector.tensor_tensor(res[:, h], out_t[h][:, :, :], dinv_of(i, h), ALU.mult).then_inc(ready[h], 1)

                    def body(i):
                        unite(i, 0)
                        if later(i):
                            finish(i - 1, 1)
                        unite(i, 1)
                        finish(i, 0)
                    over_pairs(dve, body)
                    finish(PAIRS - 1, 1)

                @block.tensor
                def _(pe):
                    def turn(i, h):
                        pe.wait_ge(united[h], united.done(i))
                        if later(i):
                            pe.wait_ge(copied[h], copied.before(i))
                        pe.sem_inc(pe_passed, 1)
                        for q in range(ROWS // 2):
                            last = nc.tensor.transpose(unit_t[h][:, q * P:(q + 1) * P],
                                                       unit[:, h, 2 * q:2 * q + 2, :].rearrange("p j d -> p (j d)"), ident[:, :])
                        last.then_inc(turned[h], 1)

                    def hide(i, h):
                        pe.wait_ge(copied[h], copied.done(i))
                        if later(i):
                            pe.wait_ge(activated[h], activated.before(i))
                        for odd in range(2):
                            k = slice(odd * D, odd * D + D)
                            last = nc.tensor.matmul(hidden_t[h][:, odd, :], w1[k, :], unit_s[k, h, :], start=True, stop=True)
                        last.then_inc(projected[h], 1)

                    def write(i, h):
                        pe.wait_ge(activated[h], activated.done(i))
                        if later(i):
                            pe.wait_ge(ready[h], ready.before(i))
                        for j in range(ROWS):
                            last = nc.tensor.matmul(out_t[h][:, j, :], hidden[:, h, j % 2, j // 2 * P:(j // 2 + 1) * P],
                                                    w2[:, :], start=True, stop=True)
                        last.then_inc(scored[h], 1)

                    def body(i):
                        turn(i, 0)
                        if later(i):
                            write(i - 1, 1)
                        hide(i, 0)
                        turn(i, 1)
                        write(i, 0)
                        hide(i, 1)
                    over_pairs(pe, body)
                    write(PAIRS - 1, 1)

                @block.scalar
                def _(act):
                    def body(i):
                        for h in range(2):
                            act.wait_ge(turned[h], turned.done(i))
                            if later(i):
                                act.wait_ge(projected[h], projected.before(i))
                            nc.scalar.activation(unit_s[:, h, :], unit_t[h][:, :], ACT.Copy).then_inc(copied[h], 1)
                            act.wait_ge(projected[h], projected.done(i))
                            if later(i):
                                act.wait_ge(scored[h], scored.before(i))
                            nc.scalar.activation(hidden[:, h], hidden_t[h][:, :, :], ACT.Relu, bias=b1[:, 0:1]).then_inc(activated[h], 1)
                    over_pairs(act, body)
            sig.end_phase()

    def first_norm_phase():
        with ExitStack() as c:
            agg = sb(c, "n1_agg", [P, 2, ROWS, D])
            own = sb(c, "n1_own", [P, 2, ROWS, D])
            before = sb(c, "n1_before", [P, 2, ROWS, D])
            both = sb(c, "n1_both", [P, 2, ROWS, D])
            conv = sb(c, "n1_conv", [P, 2, ROWS, D])
            biased = sb(c, "n1_biased", [P, 2, ROWS, D])
            total = sb(c, "n1_total", [P, 2, ROWS, D])
            loaded, stored = sig.get("nodes_loaded", 48), sig.get("nodes_stored", 16)
            added, united, summed = sig.get("node_added"), sig.get("node_united"), sig.get("node_summed")
            with_bias = sig.get("node_biased")
            norm = Norm(c)
            with nc.Block() as block:
                @block.sync
                def _(sp):
                    move_nodes(sp, [(sums, lambda h: agg[:, h]), (h_table, lambda h: own[:, h]), (x, lambda h: before[:, h])],
                               [(x1_table, lambda h: norm.out[:, h])], loaded, stored, [added, with_bias], norm.ready)

                @block.gpsimd
                def _(pool):
                    def body(i):
                        for h in range(2):
                            pool.wait_ge(loaded[h], loaded.done(i))
                            if later(i):
                                pool.wait_ge(summed[h], summed.before(i))
                            nc.gpsimd.tensor_tensor(biased[:, h], before[:, h], over_rows(b2), ALU.add).then_inc(with_bias[h], 1)
                    over_pairs(pool, body)

                @block.vector
                def _(dve):
                    def start(i, h):
                        dve.wait_ge(loaded[h], loaded.done(i))
                        if later(i):
                            dve.wait_ge(united[h], united.before(i))
                        nc.vector.tensor_tensor(both[:, h], agg[:, h], own[:, h], ALU.add).then_inc(added[h], 1)
                        dve.wait_ge(added[h], added.done(i))
                        nc.vector.tensor_tensor(conv[:, h], both[:, h], dinv_of(i, h), ALU.mult).then_inc(united[h], 1)
                        dve.wait_ge(united[h], united.done(i))
                        dve.wait_ge(with_bias[h], with_bias.done(i))
                        nc.vector.tensor_tensor(total[:, h], conv[:, h], biased[:, h], ALU.add).then_inc(summed[h], 1)
                        dve.wait_ge(summed[h], summed.done(i))
                        norm.centre(dve, i, h, total[:, h])
                    norm_steps_vector(dve, start, norm, stored)

                @block.scalar
                def _(act):
                    norm_steps_scalar(act, norm)
            sig.end_phase()

    def norm_steps_vector(dve, start, norm, stored):
        def rest(i, h):
            norm.power_of(dve, i, h)

        def body(i):
            first = not later(i)
            start(i, 0)
            if not first:
                norm.finish(dve, i - 1, 1, stored)
            rest(i, 0)
            start(i, 1)
            norm.finish(dve, i, 0, stored)
            rest(i, 1)
        over_pairs(dve, body)
        norm.finish(dve, PAIRS - 1, 1, stored)

    def norm_steps_scalar(act, norm, before=None):
        def body(i):
            for h in range(2):
                if before:
                    before(i, h)
                norm.squares(act, i, h)
                norm.deviations(act, i, h)
        over_pairs(act, body)

    def attention_norm_phase():
        with ExitStack() as c:
            agg = sb(c, "n2_agg", [P, 2, ROWS, D])
            own = sb(c, "n2_own", [P, 2, ROWS, D])
            own_s = sb(c, "n2_own_s", [P, 2, 512])
            both = sb(c, "n2_both", [P, 2, ROWS, D])
            biased = sb(c, "n2_biased", [P, 2, ROWS, D])
            total = sb(c, "n2_total", [P, 2, ROWS, D])
            own_t = [pb(c, f"n2_own_t{h}", [P, 512]) for h in range(2)]
            out_t = [pb(c, f"n2_out_t{h}", [P, 2, 512]) for h in range(2)]
            out_rows = [t[:, :, 0:ROWS // 2 * D].rearrange("p o (q d) -> p o q d", d=D) for t in out_t]

            def by_parity(t):
                return t.rearrange("p (q o) d -> p o q d", o=2)
            loaded, stored = sig.get("nodes_loaded", 32), sig.get("nodes_stored", 16)
            added, summed, with_bias = sig.get("node_added"), sig.get("node_summed"), sig.get("node_biased")
            turned, copied, projected = sig.get("rows_turned"), sig.get("rows_copied"), sig.get("projected")
            norm = Norm(c)
            with nc.Block() as block:
                @block.sync
                def _(sp):
                    move_nodes(sp, [(sums, lambda h: agg[:, h]), (x1_table, lambda h: own[:, h])],
                               [(x2_table, lambda h: norm.out[:, h])], loaded, stored, [added, turned], norm.ready)

                @block.gpsimd
                def _(pool):
                    def body(i):
                        for h in range(2):
                            pool.wait_ge(loaded[h], loaded.done(i))
                            if later(i):
                                pool.wait_ge(with_bias[h], with_bias.before(i))
                            nc.gpsimd.tensor_tensor(both[:, h], agg[:, h], own[:, h], ALU.add).then_inc(added[h], 1)
                            pool.wait_ge(added[h], added.done(i))
                            if later(i):
                                pool.wait_ge(summed[h], summed.before(i))
                            nc.gpsimd.tensor_tensor(biased[:, h], both[:, h], over_rows(res_b), ALU.add).then_inc(with_bias[h], 1)
                    over_pairs(pool, body)

                @block.tensor
                def _(pe):
                    def body(i):
                        for h in range(2):
                            pe.wait_ge(loaded[h], loaded.done(i))
                            if later(i):
                                pe.wait_ge(copied[h], copied.before(i))
                            pe.sem_inc(pe_passed, 1)
                            for q in range(ROWS // 2):
                                last = nc.tensor.transpose(own_t[h][:, q * P:(q + 1) * P],
                                                           own[:, h, 2 * q:2 * q + 2, :].rearrange("p j d -> p (j d)"), ident[:, :])
                            last.then_inc(turned[h], 1)
                            pe.wait_ge(copied[h], copied.done(i))
                            if later(i):
                                pe.wait_ge(summed[h], summed.before(i))
                            for q in range(ROWS // 2):
                                for odd in range(2):
                                    k = slice(odd * D, odd * D + D)
                                    last = nc.tensor.matmul(out_t[h][:, odd, q * D:(q + 1) * D],
                                                            own_s[k, h, q * P:(q + 1) * P], res_w[k, :], start=True, stop=True)
                            last.then_inc(projected[h], 1)
                    over_pairs(pe, body)

                @block.scalar
                def _(act):
                    def copy(i, h):
                        act.wait_ge(turned[h], turned.done(i))
                        if later(i):
                            act.wait_ge(projected[h], projected.before(i))
                        nc.scalar.activation(own_s[:, h, :], own_t[h][:, :], ACT.Copy).then_inc(copied[h], 1)
                    norm_steps_scalar(act, norm, copy)

                @block.vector
                def _(dve):
                    def start(i, h):
                        dve.wait_ge(with_bias[h], with_bias.done(i))
                        dve.wait_ge(projected[h], projected.done(i))
                        nc.vector.tensor_tensor(by_parity(total[:, h]), out_rows[h], by_parity(biased[:, h]),
                                                ALU.add).then_inc(summed[h], 1)
                        dve.wait_ge(summed[h], summed.done(i))
                        norm.centre(dve, i, h, total[:, h])
                    norm_steps_vector(dve, start, norm, stored)
            sig.end_phase()

    def relation_norm_phase():
        with ExitStack() as c:
            agg = sb(c, "n3_agg", [P, 2, ROWS, D])
            own = sb(c, "n3_own", [P, 2, ROWS, D])
            mixed = sb(c, "n3_mixed", [P, 2, ROWS, P])
            mixed_s = sb(c, "n3_mixed_s", [P, 2, ROWS, P])
            slight = sb(c, "n3_slight", [P, 2, ROWS, P])
            leaky = sb(c, "n3_leaky", [P, 2, ROWS, P])
            both = sb(c, "n3_both", [P, 2, ROWS, D])
            total = sb(c, "n3_total", [P, 2, ROWS, D])
            mixed_t = [pb(c, f"n3_mixed_t{h}", [P, ROWS, P]) for h in range(2)]
            out_t = [pb(c, f"n3_out_t{h}", [P, ROWS, P]) for h in range(2)]
            loaded, stored = sig.get("nodes_loaded", 32), sig.get("nodes_stored", 16)
            added, summed, united = sig.get("node_added"), sig.get("node_summed"), sig.get("node_united")
            turned, copied, projected = sig.get("rows_turned"), sig.get("rows_copied"), sig.get("projected")
            slighted, leaked, multiplied = sig.get("activated"), sig.get("node_result"), sig.get("node_biased")
            norm = Norm(c)
            with nc.Block() as block:
                @block.sync
                def _(sp):
                    move_nodes(sp, [(sums, lambda h: agg[:, h]), (x2_table, lambda h: own[:, h])],
                               [(x3_table, lambda h: norm.out[:, h])], loaded, stored, [added, multiplied, summed], norm.ready)

                @block.gpsimd
                def _(pool):
                    def body(i):
                        for h in range(2):
                            pool.wait_ge(loaded[h], loaded.done(i))
                            if later(i):
                                pool.wait_ge(turned[h], turned.before(i))
                            nc.gpsimd.tensor_tensor(mixed[:, h, :, 0:D], agg[:, h], own[:, h], ALU.add).then_inc(added[h], 1)
                            nc.gpsimd.tensor_tensor(mixed[:, h, :, D:P], agg[:, h], own[:, h], ALU.mult).then_inc(multiplied[h], 1)
                    over_pairs(pool, body)

                @block.tensor
                def _(pe):
                    def turn(i, h):
                        pe.wait_ge(added[h], added.done(i))
                        pe.wait_ge(multiplied[h], multiplied.done(i))
                        if later(i):
                            pe.wait_ge(copied[h], copied.before(i))
                        pe.sem_inc(pe_passed, 1)
                        for j in range(ROWS):
                            last = nc.tensor.transpose(mixed_t[h][:, j, :], mixed[:, h, j, :], ident[:, :])
                        last.then_inc(turned[h], 1)

                    def write(i, h):
                        pe.wait_ge(copied[h], copied.done(i))
                        if later(i):
                            pe.wait_ge(slighted[h], slighted.before(i))
                            pe.wait_ge(leaked[h], leaked.before(i))
                        for j in range(ROWS):
                            last = nc.tensor.matmul(out_t[h][:, j, :], mixed_s[:, h, j, :], fc2[:, :], start=True, stop=True)
                        last.then_inc(projected[h], 1)

                    def body(i):
                        turn(i, 0)
                        if later(i):
                            write(i - 1, 1)
                        turn(i, 1)
                        write(i, 0)
                    over_pairs(pe, body)
                    write(PAIRS - 1, 1)

                @block.scalar
                def _(act):
                    def copy(i, h):
                        act.wait_ge(turned[h], turned.done(i))
                        if later(i):
                            act.wait_ge(projected[h], projected.before(i))
                        nc.scalar.activation(mixed_s[:, h], mixed_t[h][:, :, :], ACT.Copy).then_inc(copied[h], 1)

                    def slight_of(i, h):
                        act.wait_ge(projected[h], projected.done(i))
                        if later(i):
                            act.wait_ge(leaked[h], leaked.before(i))
                        nc.scalar.activation(slight[:, h], out_t[h][:, :, :], ACT.Copy, scale=0.01).then_inc(slighted[h], 1)

                    def body(i):
                        first = not later(i)
                        copy(i, 0)
                        if not first:
                            slight_of(i - 1, 1)
                            norm.squares(act, i - 1, 1)
                            norm.deviations(act, i - 1, 1)
                        copy(i, 1)
                        slight_of(i, 0)
                        norm.squares(act, i, 0)
                        norm.deviations(act, i, 0)
                    over_pairs(act, body)
                    slight_of(PAIRS - 1, 1)
                    norm.squares(act, PAIRS - 1, 1)
                    norm.deviations(act, PAIRS - 1, 1)

                @block.vector
                def _(dve):
                    def start(i, h):
                        dve.wait_ge(slighted[h], slighted.done(i))
                        if later(i):
                            dve.wait_ge(united[h], united.before(i))
                        nc.vector.tensor_tensor(leaky[:, h], out_t[h][:, :, :], slight[:, h], ALU.max).then_inc(leaked[h], 1)
                        dve.wait_ge(leaked[h], leaked.done(i))
                        nc.vector.tensor_tensor(both[:, h], leaky[:, h, :, 0:D], leaky[:, h, :, D:P], ALU.add).then_inc(united[h], 1)
                        dve.wait_ge(united[h], united.done(i))
                        dve.wait_ge(loaded[h], loaded.done(i))
                        nc.vector.tensor_tensor(total[:, h], both[:, h], own[:, h], ALU.add).then_inc(summed[h], 1)
                        dve.wait_ge(summed[h], summed.done(i))
                        norm.centre(dve, i, h, total[:, h])
                    norm_steps_vector(dve, start, norm, stored)
            sig.end_phase()

    def update_norm_phase():
        with ExitStack() as c:
            pair = sb(c, "n4_pair", [P, 2, ROWS, P])
            pair_s = sb(c, "n4_pair_s", [P, 2, ROWS * P])
            hidden = sb(c, "n4_hidden", [HID, 2, ROWS * P])
            biased = sb(c, "n4_biased", [P, 2, ROWS, D])
            total = sb(c, "n4_total", [P, 2, ROWS, D])
            pair_t = [pb(c, f"n4_pair_t{h}", [P, 512]) for h in range(2)]
            hidden_t = [pb(c, f"n4_hidden_t{h}", [HID, 1024]) for h in range(2)]
            out_t = [pb(c, f"n4_out_t{h}", [P, ROWS, D]) for h in range(2)]
            loaded, stored = sig.get("nodes_loaded", 32), sig.get("nodes_stored", 16)
            summed, with_bias = sig.get("node_summed"), sig.get("node_biased")
            turned, copied, projected = sig.get("rows_turned", 2), sig.get("rows_copied", 2), sig.get("projected")
            activated, written = sig.get("activated"), sig.get("scored")
            norm = Norm(c)
            with nc.Block() as block:
                @block.sync
                def _(sp):
                    move_nodes(sp, [(x3_table, lambda h: pair[:, h, :, 0:D]), (sums, lambda h: pair[:, h, :, D:P])],
                               [(out, lambda h: norm.out[:, h])], loaded, stored, [turned, with_bias], norm.ready)

                @block.gpsimd
                def _(pool):
                    def body(i):
                        for h in range(2):
                            pool.wait_ge(loaded[h], loaded.done(i))
                            if later(i):
                                pool.wait_ge(summed[h], summed.before(i))
                            nc.gpsimd.tensor_tensor(biased[:, h], pair[:, h, :, 0:D], over_rows(u_b2), ALU.add).then_inc(with_bias[h], 1)
                    over_pairs(pool, body)

                @block.tensor
                def _(pe):
                    def turn(i, h):
                        pe.wait_ge(loaded[h], loaded.done(i))
                        if h or later(i):
                            pe.wait_ge(copied[1 - h], copied.previous(i, h))
                        pe.sem_inc(pe_passed, 1)
                        for k in range(2):
                            for j in range(4):
                                last = nc.tensor.transpose(pair_t[k][:, j * P:(j + 1) * P], pair[:, h, 4 * k + j, :], ident[:, :])
                            last.then_inc(turned[h], 1)

                    def hide(i, h):
                        pe.wait_ge(copied[h], copied.done(i))
                        if later(i):
                            pe.wait_ge(activated[h], activated.before(i))
                        for k in range(2):
                            last = nc.tensor.matmul(hidden_t[h][:, k * 512:(k + 1) * 512], u_w1[:, :],
                                                    pair_s[:, h, k * 512:(k + 1) * 512], start=True, stop=True)
                        last.then_inc(projected[h], 1)

                    def write(i, h):
                        pe.wait_ge(activated[h], activated.done(i))
                        if later(i):
                            pe.wait_ge(summed[h], summed.before(i))
                        for j in range(ROWS):
                            last = nc.tensor.matmul(out_t[h][:, j, :], hidden[:, h, j * P:(j + 1) * P], u_w2[:, :],
                                                    start=True, stop=True)
                        last.then_inc(written[h], 1)

                    def body(i):
                        turn(i, 0)
                        if later(i):
                            write(i - 1, 1)
                        hide(i, 0)
                        turn(i, 1)
                        write(i, 0)
                        hide(i, 1)
                    over_pairs(pe, body)
                    write(PAIRS - 1, 1)

                @block.scalar
                def _(act):
                    def copy(i, h):
                        if later(i):
                            act.wait_ge(projected[h], projected.before(i))
                        for k in range(2):
                            act.wait_ge(turned[h], i * 2 + (turned.base + k + 1))
                            nc.scalar.activation(pair_s[:, h, k * 512:(k + 1) * 512], pair_t[k][:, :], ACT.Copy).then_inc(copied[h], 1)

                    def rectify(i, h):
                        act.wait_ge(projected[h], projected.done(i))
                        if later(i):
                            act.wait_ge(written[h], written.before(i))
                        nc.scalar.activation(hidden[:, h, :], hidden_t[h][:, :], ACT.Relu, bias=u_b1[:, 0:1]).then_inc(activated[h], 1)

                    def body(i):
                        first = not later(i)
                        copy(i, 0)
                        if not first:
                            norm.squares(act, i - 1, 1)
                            norm.deviations(act, i - 1, 1)
                        rectify(i, 0)
                        copy(i, 1)
                        norm.squares(act, i, 0)
                        norm.deviations(act, i, 0)
                        rectify(i, 1)
                    over_pairs(act, body)
                    norm.squares(act, PAIRS - 1, 1)
                    norm.deviations(act, PAIRS - 1, 1)

                @block.vector
                def _(dve):
                    def start(i, h):
                        dve.wait_ge(with_bias[h], with_bias.done(i))
                        dve.wait_ge(written[h], written.done(i))
                        nc.vector.tensor_tensor(total[:, h], out_t[h][:, :, :], biased[:, h], ALU.add).then_inc(summed[h], 1)
                        dve.wait_ge(summed[h], summed.done(i))
                        norm.centre(dve, i, h, total[:, h])
                    norm_steps_vector(dve, start, norm, stored)
            sig.end_phase()

    scale_phase()
    sum_phase(y_table)
    gcn_phase()
    sum_phase(h_table)
    first_norm_phase()
    attention_phase(x1_table, relations=False)
    attention_norm_phase()
    attention_phase(x2_table, relations=True)
    relation_norm_phase()
    message_phase(x3_table)
    update_norm_phase()


_INS = ["x", "src", "dst", "edge_attr_32", "edge_attr_64", "edge_type_10", "L0_gnn_W1", "L0_gnn_b1", "L0_gnn_W2",
        "L0_gnn_b2", "L1_gnn_W_out", "L1_gnn_b_out", "L1_gnn_attn_w", "L1_gnn_res_W", "L1_gnn_res_b",
        "L2_gnn_relation_weight", "L2_gnn_res_fc_w", "L2_gnn_res_fc2_w", "L3_gnn_mW1", "L3_gnn_mb1", "L3_gnn_mW2",
        "L3_gnn_mb2", "L3_gnn_uW1", "L3_gnn_ub1", "L3_gnn_uW2", "L3_gnn_ub2"]


def kernel(**inputs):
    import numpy as _np
    import concourse.bacc as _bacc
    from concourse import mybir as _mybir
    from concourse.bass_utils import run_bass_kernel_spmd as _run

    nc = _bacc.Bacc("TRN2", target_bir_lowering=False, num_devices=1)
    arrays, args = {}, {}
    for name in _INS:
        a = _np.ascontiguousarray(inputs[name])
        arrays[f"in_{name}_dram"] = a
        args[name] = nc.dram_tensor(f"in_{name}_dram", a.shape, _mybir.dt.from_np(a.dtype), kind="ExternalInput").ap()
    out = nc.dram_tensor("out_dram", (NODES, D), F32, kind="ExternalOutput").ap()
    bass_gnn(nc, args, out)
    r = _run(nc, [arrays], core_ids=[0])
    return r.results[0]["out_dram"]
```

```python
from contextlib import ExitStack

import concourse.bass as bass
from concourse import mybir

F32 = mybir.dt.float32
BF16 = mybir.dt.bfloat16
FP16 = mybir.dt.float16
I32 = mybir.dt.int32
ALU = mybir.AluOpType
ACT = mybir.ActivationFunctionType
AX_X = mybir.AxisListType.X

P = 128
NODES = 100000
EDGES = 50000
D = 64
HID = 128
DE = 32
RELS = 10
EPS = 1e-5

ROWS = 8
NODE_BLOCK = P * ROWS
NODE_BLOCKS = -(-NODES // NODE_BLOCK)
NODE_TAIL = (NODES - (NODE_BLOCKS - 1) * NODE_BLOCK) // ROWS

TILES = 4
EDGE_BLOCK = TILES * P
EDGE_BLOCKS = -(-EDGES // EDGE_BLOCK)
EDGE_TILES = -(-EDGES // P)
BLOCKS = NODE_BLOCKS
DEEP = 4
assert BLOCKS % 2 == 0
assert NODE_BLOCKS == EDGE_BLOCKS and NODE_TAIL * ROWS == NODES % NODE_BLOCK
CHUNKS = -(-EDGE_BLOCKS * TILES // P)

ZERO_PARTS, ZERO_WIDTH = 80, 4000
NOWHERE = 200000
LOW = -1.0e30


class At:

    def __init__(self, i, k):
        self.i, self.k, self.h = i, k, k % 2

    def __sub__(self, n):
        groups, k = divmod(self.k - n, DEEP)
        return At(self.i + groups if groups else self.i, k)

    def times(self, n):
        return self.i * (DEEP * n) + self.k * n

    @property
    def static(self):
        return isinstance(self.i, int)

    @property
    def exists(self):
        return not self.static or 0 <= self.i * DEEP + self.k < BLOCKS

    @property
    def is_last(self):
        return self.static and self.i * DEEP + self.k == BLOCKS - 1


class Signal:

    def __init__(self, ctx, nc, name):
        self.sem = ctx.enter_context(nc.semaphore(name))
        self.base, self.step = 0, 1

    def __getitem__(self, at):
        return self.sem

    def part(self, at, n):
        return at.times(self.step) + (self.base + n)

    def done(self, at):
        return self.part(at, self.step)

    def end_phase(self):
        self.base += self.step * BLOCKS


class Landing:

    def __init__(self, ctx, nc, name):
        self.sems = [ctx.enter_context(nc.semaphore(f"{name}_{k}")) for k in range(DEEP)]
        self.base, self.step = [0] * DEEP, 16

    def __getitem__(self, at):
        return self.sems[at.k]

    def done(self, at):
        return at.i * self.step + (self.base[at.k] + self.step)

    def end_phase(self):
        self.base = [b + self.step * len(range(k, BLOCKS, DEEP)) for k, b in enumerate(self.base)]


class Signals:
    def __init__(self, ctx, nc):
        self.ctx, self.nc, self.made, self.used = ctx, nc, {}, []
        self.phase = 0

    def get(self, name, step=1, kind=Signal):
        if name not in self.made:
            self.made[name] = kind(self.ctx, self.nc, name)
        signal = self.made[name]
        signal.step = step
        self.used.append(signal)
        return signal

    def landing(self, name, step):
        return self.get(name, step, Landing)

    def end_phase(self):
        for signal in self.used:
            signal.end_phase()
        self.used = []
        self.phase += 1


def over_blocks(eng, *stages):
    last_lag = max(lag for _, lag in stages)
    first = 1 + -(-last_lag // DEEP)

    def turn(at):
        for stage, lag in stages:
            if (at - lag).exists:
                stage(at - lag)

    for b in range(first * DEEP):
        turn(At(b // DEEP, b % DEEP))
    with eng.Fori(first, BLOCKS // DEEP) as i:
        for k in range(DEEP):
            turn(At(i, k))
    for b in range(BLOCKS // DEEP * DEEP, BLOCKS + last_lag):
        turn(At(b // DEEP, b % DEEP))


def last_blocks():
    return [At(b // DEEP, b % DEEP) for b in range(BLOCKS - DEEP, BLOCKS)]


def bass_gnn(nc, ins, out):
    with ExitStack() as ctx:
        build(nc, ctx, ins, out)


def build(nc, ctx, ins, out):
    sig = Signals(ctx, nc)

    def sem(name):
        return ctx.enter_context(nc.semaphore(name))

    def sb(c, name, shape, dt=F32):
        return c.enter_context(nc.sbuf_tensor(f"{name}_{sig.phase}", shape, dt))

    def pb(c, name, shape):
        return c.enter_context(nc.psum_tensor(f"{name}_{sig.phase}", shape, F32))

    def table(name):
        return nc.dram_tensor(name, (NODES, D), F32, kind="Internal").ap()

    x = ins["x"]
    y_table = table("scaled_x")
    h_table = table("scaled_h")
    x1_table = table("x_after_gcn")
    x2_table = table("x_after_attention")
    x3_table = table("x_after_relations")
    sums = table("sums_by_dst")
    same_flags = nc.dram_tensor("same_run_flags", (EDGE_BLOCKS * EDGE_BLOCK + 1,), BF16, kind="Internal").ap()

    ident = sb(ctx, "ident", [P, P])
    ones = sb(ctx, "ones", [P, P])
    edge_idx = sb(ctx, "edge_idx", [P, 2, CHUNKS * P], I32)
    src_idx, dst_idx = edge_idx[:, 0, :], edge_idx[:, 1, :]
    dst_raw = sb(ctx, "dst_raw", [P, CHUNKS * P], I32)
    put_idx = sb(ctx, "put_idx", [P, CHUNKS * P], I32)
    dinv = sb(ctx, "dinv", [P, NODE_BLOCKS * ROWS])
    eps = sb(ctx, "eps", [P, 1])
    zeros = sb(ctx, "zeros", [P, ZERO_WIDTH])

    w1 = sb(ctx, "w1", [P, HID])
    b1 = sb(ctx, "b1", [HID, 1])
    w2_pair = sb(ctx, "w2_pair", [HID, 2, P])
    b2 = sb(ctx, "b2", [P, D])
    w_out2 = sb(ctx, "w_out2", [P, P])
    b_out2 = sb(ctx, "b_out2", [P, 1])
    attn_col = sb(ctx, "attn_col", [P, 1])
    attn_all = sb(ctx, "attn_all", [P, P])
    res_w = sb(ctx, "res_w", [P, P])
    res_b = sb(ctx, "res_b", [P, D])
    rel2 = sb(ctx, "rel2", [P, RELS, P])
    fc_raw = sb(ctx, "fc_raw", [D, 2, D])
    fc2 = sb(ctx, "fc2", [P, P])
    m_w1 = sb(ctx, "m_w1", [P, HID])
    m_w1e = sb(ctx, "m_w1e", [DE, HID])
    m_b1 = sb(ctx, "m_b1", [HID, 1])
    m_w2 = sb(ctx, "m_w2", [HID, D])
    m_b2 = sb(ctx, "m_b2", [D, 1])
    u_w1 = sb(ctx, "u_w1", [P, HID])
    u_b1 = sb(ctx, "u_b1", [HID, 1])
    u_w2 = sb(ctx, "u_w2", [HID, D])
    u_b2 = sb(ctx, "u_b2", [P, D])

    pe_passed, pool_passed, sp_passed = sem("pe_passed"), sem("pool_passed"), sem("sp_passed")
    ident_set = sem("ident_set")
    index_steps = sem("index_steps")

    def column(v):
        return v.rearrange("(d a) -> d a", a=1)

    def every_partition(v):
        return v.partition_broadcast(P)

    with ExitStack() as c:
        dst_rows = sb(c, "dst_rows", [P, CHUNKS, P], I32)
        next_rows = sb(c, "next_rows", [P, CHUNKS, P], I32)
        src_rows = sb(c, "src_rows", [P, CHUNKS, P], I32)
        rows_f = sb(c, "rows_f", [P, 3, CHUNKS, P])
        same_f = sb(c, "same_f", [P, CHUNKS, P])
        same_b = sb(c, "same_b", [P, CHUNKS, P], BF16)
        zero_b = sb(c, "zero_b", [1, 1], BF16)
        real = sb(c, "real", [P, CHUNKS * P])
        turned = [pb(c, f"turned{k}", [P, CHUNKS * P]) for k in range(3)]
        fc_t = pb(c, "fc_t", [D, 2, D])

        cleared = sem("cleared")
        pads_set = sem("pads_set")
        weights_in = sem("weights_in")
        rows_in = sem("rows_in")
        zeros_set = sem("zeros_set")
        prep = index_steps
        flags_made = sem("flags_made")
        flags_out = sem("flags_out")
        zeroed = sem("sums_zeroed")
        rows_turned = sem("index_rows_turned")
        fc_turned = sem("fc_turned")
        weights_spread = sem("weights_spread")

        WEIGHT_LOADS = 27
        full_rows = EDGES // P
        main = (CHUNKS - 1) * P
        extra = full_rows - main

        def load_rows(eng, to, vec, shift):
            n = EDGES - shift
            tail = n - full_rows * P
            eng.dma_start(to[:, 0:CHUNKS - 1, :],
                          vec[shift:shift + main * P].rearrange("(c r p) -> r c p", r=P, p=P)).then_inc(rows_in, 16)
            eng.dma_start(to[0:extra, CHUNKS - 1, :],
                          vec[shift + main * P:shift + full_rows * P].rearrange("(r p) -> r p", p=P)).then_inc(rows_in, 16)
            eng.dma_start(to[extra:extra + 1, CHUNKS - 1, 0:tail],
                          vec[shift + full_rows * P:EDGES].rearrange("(a p) -> a p", a=1)).then_inc(rows_in, 16)

        with nc.Block() as block:
            @block.gpsimd
            def _(pool):
                nc.gpsimd.memset(dst_rows[:, :, :], NOWHERE).then_inc(pads_set, 1)
                nc.gpsimd.memset(next_rows[:, :, :], -1).then_inc(pads_set, 1)
                nc.gpsimd.memset(src_rows[:, :, :], 0).then_inc(pads_set, 1)
                nc.gpsimd.memset(ident[:, :], 0.0).then_inc(ident_set, 1)
                pool.wait_ge(ident_set, 1)
                nc.gpsimd.affine_select(out=ident[:, :], in_=ident[:, :], compare_op=ALU.not_equal, fill=1.0,
                                        base=0, pattern=[[-1, P]], channel_multiplier=1).then_inc(ident_set, 1)

            @block.sync
            def _(sp):
                sp.wait_ge(pads_set, 3)
                load_rows(sp, dst_rows, ins["dst"], 0)
                load_rows(sp, next_rows, ins["dst"], 1)
                load_rows(sp, src_rows, ins["src"], 0)
                sp.wait_ge(cleared, 8)
                moves = [
                    (w1[0:D, :], ins["L0_gnn_W1"]), (w1[D:P, :], ins["L0_gnn_W1"]),
                    (b1[:, :], column(ins["L0_gnn_b1"])), (w2_pair[:, 0, 0:D], ins["L0_gnn_W2"]), (w2_pair[:, 1, D:P], ins["L0_gnn_W2"]),
                    (b2[:, :], every_partition(ins["L0_gnn_b2"])),
                    (w_out2[0:D, 0:D], ins["L1_gnn_W_out"]), (w_out2[D:P, D:P], ins["L1_gnn_W_out"]),
                    (b_out2[0:D, :], column(ins["L1_gnn_b_out"])), (b_out2[D:P, :], column(ins["L1_gnn_b_out"])),
                    (attn_col[:, :], column(ins["L1_gnn_attn_w"])),
                    (res_w[0:D, 0:D], ins["L1_gnn_res_W"]), (res_w[D:P, D:P], ins["L1_gnn_res_W"]),
                    (res_b[:, :], every_partition(ins["L1_gnn_res_b"])),
                    (rel2[0:D, :, 0:D], ins["L2_gnn_relation_weight"].rearrange("r i o -> i r o")),
                    (rel2[D:P, :, D:P], ins["L2_gnn_relation_weight"].rearrange("r i o -> i r o")),
                    (fc_raw[:, 0, :], ins["L2_gnn_res_fc_w"]), (fc_raw[:, 1, :], ins["L2_gnn_res_fc2_w"]),
                    (m_w1[:, :], ins["L3_gnn_mW1"][0:P, :]), (m_w1e[:, :], ins["L3_gnn_mW1"][P:P + DE, :]),
                    (m_b1[:, :], column(ins["L3_gnn_mb1"])), (m_w2[:, :], ins["L3_gnn_mW2"]),
                    (m_b2[:, :], column(ins["L3_gnn_mb2"])),
                    (u_w1[:, :], ins["L3_gnn_uW1"]), (u_b1[:, :], column(ins["L3_gnn_ub1"])),
                    (u_w2[:, :], ins["L3_gnn_uW2"]), (u_b2[:, :], every_partition(ins["L3_gnn_ub2"])),
                ]
                assert len(moves) == WEIGHT_LOADS
                for to, of in moves:
                    sp.dma_start(to, of).then_inc(weights_in, 16)
                sp.wait_ge(flags_made, 2)
                sp.dma_start(same_flags[1:1 + main * P].rearrange("(c r p) -> r c p", r=P, p=P),
                             same_b[:, 0:CHUNKS - 1, :]).then_inc(flags_out, 16)
                left = EDGE_BLOCKS * TILES - main
                sp.dma_start(same_flags[1 + main * P:1 + (main + left) * P].rearrange("(r p) -> r p", p=P),
                             same_b[0:left, CHUNKS - 1, :]).then_inc(flags_out, 16)
                sp.dma_start(same_flags[0:1].rearrange("(a p) -> a p", a=1), zero_b[:, :]).then_inc(flags_out, 16)
                sp.wait_ge(flags_out, 48)
                sp.wait_ge(weights_in, 16 * WEIGHT_LOADS)

            @block.tensor
            def _(pe):
                pe.wait_ge(ident_set, 2)
                pe.wait_ge(prep, 5)
                for a in range(3):
                    for k in range(CHUNKS):
                        last = nc.tensor.transpose(turned[a][:, k * P:(k + 1) * P], rows_f[:, a, k, :], ident[:, :])
                last.then_inc(rows_turned, 1)
                pe.wait_ge(weights_in, 16 * WEIGHT_LOADS)
                for k in range(2):
                    last = nc.tensor.transpose(fc_t[:, k, :], fc_raw[:, k, :], ident[0:D, 0:D])
                last.then_inc(fc_turned, 1)

            @block.vector
            def _(dve):
                nc.vector.memset(ones[:, :], 1.0).then_inc(cleared, 1)
                nc.vector.memset(w_out2[:, :], 0.0).then_inc(cleared, 1)
                nc.vector.memset(rel2[:, :, :], 0.0).then_inc(cleared, 1)
                nc.vector.memset(fc2[:, :], 0.0).then_inc(cleared, 1)
                nc.vector.memset(res_w[:, :], 0.0).then_inc(cleared, 1)
                nc.vector.memset(w2_pair[:, :, :], 0.0).then_inc(cleared, 1)
                nc.vector.memset(eps[:, :], EPS).then_inc(cleared, 1)
                nc.vector.memset(zero_b[:, :], 0.0).then_inc(cleared, 1)
                nc.vector.memset(zeros[:, :], 0.0).then_inc(zeros_set, 1)
                dve.wait_ge(rows_in, 16 * 9)
                nc.vector.tensor_tensor(same_f[:, :, :], dst_rows[:, :, :], next_rows[:, :, :], ALU.is_equal).then_inc(prep, 1)
                nc.vector.tensor_copy(rows_f[:, 0], src_rows[:, :, :]).then_inc(prep, 1)
                nc.vector.tensor_copy(rows_f[:, 1], dst_rows[:, :, :]).then_inc(prep, 1)
                dve.wait_ge(prep, 3)
                dve.wait_ge(cleared, 8)
                nc.vector.tensor_copy(same_b[:, :, :], same_f[:, :, :]).then_inc(flags_made, 2)
                nc.vector.scalar_tensor_tensor(out=rows_f[:, 2], in0=same_f[:, :, :], scalar=float(NOWHERE),
                                               in1=rows_f[:, 1], op0=ALU.mult, op1=ALU.add).then_inc(prep, 2)
                dve.wait_ge(rows_turned, 1)
                nc.vector.tensor_copy(src_idx[:, :], turned[0][:, :]).then_inc(prep, 1)
                nc.vector.tensor_copy(put_idx[:, :], turned[2][:, :]).then_inc(prep, 1)
                nc.vector.tensor_scalar(real[:, :], turned[1][:, :], float(NODES), None, ALU.is_lt).then_inc(prep, 1)
                nc.vector.tensor_copy(dst_raw[:, :], turned[1][:, :]).then_inc(prep, 1)
                dve.wait_ge(prep, 9)
                nc.vector.tensor_tensor(dst_idx[:, :], turned[1][:, :], real[:, :], ALU.mult).then_inc(prep, 1)
                dve.wait_ge(fc_turned, 1)
                nc.vector.tensor_copy(fc2[0:D, 0:D], fc_t[:, 0, :]).then_inc(weights_spread, 1)
                nc.vector.tensor_copy(fc2[D:P, D:P], fc_t[:, 1, :]).then_inc(weights_spread, 1)
                nc.vector.tensor_scalar(attn_all[:, :], ones[:, :], attn_col[:, 0:1], None, ALU.mult).then_inc(weights_spread, 1)

    with ExitStack() as c:
        COLS = NODE_BLOCKS * ROWS
        HALF = 512
        number = sb(c, "number", [P, COLS], I32)
        number_h = sb(c, "number_h", [P, COLS], FP16)
        hi = sb(c, "hi", [P, EDGE_TILES + 1], I32)
        lo = sb(c, "lo", [P, EDGE_TILES + 1], I32)
        mid = sb(c, "mid", [P, EDGE_TILES + 1], I32)
        col_f = sb(c, "col_f", [P, EDGE_TILES + 1])
        part_f = sb(c, "part_f", [P, EDGE_TILES + 1])
        is_part = sb(c, "is_part", [P, DEEP, P], FP16)
        is_col = sb(c, "is_col", [P, DEEP, COLS], FP16)
        root = sb(c, "root", [P, COLS])
        counts = pb(c, "counts", [P, 1024])
        numbered = sem("numbered")
        split = sem("nodes_split")
        hot = [sem(f"one_hot_{k}") for k in range(DEEP)]
        counted = [sem(f"counted_{k}") for k in range(DEEP)]
        rooted = sem("rooted")
        inverted = sem("inverted")
        LOOPS = EDGE_TILES // DEEP
        LEFT = EDGE_TILES % DEEP
        with nc.Block() as block:
            @block.gpsimd
            def _(pool):
                nc.gpsimd.iota(number[:, :], [[1, COLS]], base=0, channel_multiplier=0).then_inc(numbered, 1)

            @block.vector
            def _(dve):
                T = EDGE_TILES + 1
                node = dst_raw[:, 0:T]
                nc.vector.tensor_scalar(hi[:, :], node, 10, 3, ALU.arith_shift_right, ALU.logical_shift_left).then_inc(split, 1)
                nc.vector.tensor_scalar(lo[:, :], node, 7, None, ALU.bitwise_and).then_inc(split, 1)
                dve.wait_ge(split, 2)
                nc.vector.tensor_tensor(col_f[:, :], hi[:, :], lo[:, :], ALU.add).then_inc(split, 1)
                nc.vector.tensor_scalar(mid[:, :], node, 3, 127, ALU.arith_shift_right, ALU.bitwise_and).then_inc(split, 1)
                dve.wait_ge(split, 4)
                nc.vector.tensor_copy(part_f[:, :], mid[:, :]).then_inc(split, 1)
                dve.wait_ge(numbered, 1)
                nc.vector.tensor_copy(number_h[:, :], number[:, :]).then_inc(split, 1)
                dve.wait_ge(split, 6)

                def one_hot(t, h, before):
                    if before is not None:
                        dve.wait_ge(counted[h], before)
                    nc.vector.tensor_scalar(is_part[:, h], number_h[:, 0:P], part_f[:, bass.ds(t, 1)], None,
                                            ALU.is_equal).then_inc(hot[h], 1)
                    nc.vector.tensor_scalar(is_col[:, h], number_h[:, :], col_f[:, bass.ds(t, 1)], None,
                                            ALU.is_equal).then_inc(hot[h], 1)
                for k in range(DEEP):
                    one_hot(k, k, None)
                with dve.Fori(1, LOOPS) as i:
                    for k in range(DEEP):
                        one_hot(DEEP * i + k, k, i)
                for k in range(LEFT):
                    one_hot(DEEP * LOOPS + k, k, LOOPS)
                dve.wait_ge(rooted, 1)
                nc.vector.reciprocal(dinv[:, :], root[:, :]).then_inc(inverted, 1)

            @block.tensor
            def _(pe):
                def count(h, done, start, stop):
                    pe.wait_ge(hot[h], done)
                    nc.tensor.matmul(counts[:, 0:HALF], is_part[:, h], is_col[:, h, 0:HALF], start=start, stop=stop)
                    nc.tensor.matmul(counts[:, HALF:COLS], is_part[:, h], is_col[:, h, HALF:COLS],
                                     start=start, stop=stop).then_inc(counted[h], 1)
                for k in range(DEEP):
                    count(k, 2, k == 0, False)
                with pe.Fori(1, LOOPS) as i:
                    for k in range(DEEP):
                        count(k, 2 * i + 2, False, False)
                for k in range(LEFT):
                    count(k, 2 * LOOPS + 2, False, k == LEFT - 1)

            @block.scalar
            def _(act):
                act.wait_ge(zeros_set, 1)
                flat_sums = sums.rearrange("(p r) d -> p (r d)", p=ZERO_PARTS)
                moves = NODES * D // ZERO_PARTS // ZERO_WIDTH
                for k in range(moves):
                    act.dma_start(flat_sums[:, k * ZERO_WIDTH:(k + 1) * ZERO_WIDTH], zeros[0:ZERO_PARTS, :]).then_inc(zeroed, 16)
                act.wait_ge(zeroed, 16 * moves)
                act.wait_ge(counted[LEFT - 1], LOOPS + 1)
                nc.scalar.activation(root[:, 0:COLS], counts[:, 0:COLS], ACT.Sqrt, bias=ones[:, 0:1]).then_inc(rooted, 1)

    def node_rows(t, at):
        if at.is_last:
            return t[(BLOCKS - 1) * NODE_BLOCK:NODES, :].rearrange("(p j) d -> p j d", j=ROWS)
        return t[bass.ds(at.times(NODE_BLOCK), NODE_BLOCK), :].rearrange("(p j) d -> p j d", j=ROWS)

    def node_parts(at):
        return NODE_TAIL if at.is_last else P

    def load_nodes(sp, at, moves, loaded):
        sp.sem_inc(sp_passed, 1)
        for t, buf in moves:
            sp.dma_start(buf[0:node_parts(at)], node_rows(t, at)).then_inc(loaded[at], 16)

    def store_nodes(sp, at, t, buf, ready, stored):
        sp.wait_ge(ready[at], ready.done(at))
        sp.sem_inc(sp_passed, 1)
        sp.dma_start(node_rows(t, at), buf[0:node_parts(at)]).then_inc(stored[at], 16)

    def wait_stored(sp, stored):
        for at in last_blocks():
            sp.wait_ge(stored[at], stored.done(at))

    def dinv_of(at):
        return dinv[:, bass.ds(at.times(ROWS), ROWS)].unsqueeze(2).to_broadcast([P, ROWS, D])

    def over_rows(v):
        return v[:, :].unsqueeze(1).to_broadcast([P, ROWS, D])

    def of_row(v):
        return v.unsqueeze(2).to_broadcast([P, ROWS, D])

    class Norm:

        def __init__(self, c, scalar_sums=False):
            self.scalar_sums = scalar_sums
            self.total = sb(c, "norm_total", [P, DEEP, ROWS])
            self.centred = sb(c, "norm_centred", [P, DEEP, ROWS, D])
            self.square = sb(c, "norm_square", [P, DEEP, ROWS, D])
            self.power = sb(c, "norm_power", [P, DEEP, ROWS])
            self.deviation = sb(c, "norm_deviation", [P, DEEP, ROWS])
            self.scale = sb(c, "norm_scale", [P, DEEP, ROWS])
            self.out = sb(c, "norm_out", [P, DEEP, ROWS, D])
            self.totalled, self.shifted = sig.get("totalled"), sig.get("shifted")
            self.powered = sig.get("powered")
            if not scalar_sums:
                self.squared = sig.get("squared")
            self.rooted, self.scaled, self.ready = sig.get("deviated"), sig.get("scale_made"), sig.get("normed")

        def add_up(self, dve, at, rows):
            nc.vector.tensor_reduce(self.total[:, at.k], rows, AX_X, ALU.add).then_inc(self.totalled[at], 1)

        def centre(self, dve, at, rows):
            dve.wait_ge(self.totalled[at], self.totalled.done(at))
            if (at - DEEP).exists:
                dve.wait_ge(self.ready[at - DEEP], self.ready.done(at - DEEP))
            nc.vector.scalar_tensor_tensor(out=self.centred[:, at.k], in0=of_row(self.total[:, at.k]), scalar=-1.0 / D,
                                           in1=rows, op0=ALU.mult, op1=ALU.add).then_inc(self.shifted[at], 1)

        def squares(self, act, at):
            act.wait_ge(self.shifted[at], self.shifted.done(at))
            if self.scalar_sums:
                if (at - DEEP).exists:
                    act.wait_ge(self.rooted[at - DEEP], self.rooted.done(at - DEEP))
                for j in range(ROWS):
                    last = nc.scalar.activation(self.square[:, at.k, j, :], self.centred[:, at.k, j, :], ACT.Square,
                                                accum_out=self.power[:, at.k, j:j + 1])
                last.then_inc(self.powered[at], 1)
                return
            if (at - DEEP).exists:
                act.wait_ge(self.powered[at - DEEP], self.powered.done(at - DEEP))
            nc.scalar.activation(self.square[:, at.k], self.centred[:, at.k], ACT.Square).then_inc(self.squared[at], 1)

        def power_of(self, dve, at):
            dve.wait_ge(self.squared[at], self.squared.done(at))
            nc.vector.tensor_reduce(self.power[:, at.k], self.square[:, at.k], AX_X, ALU.add).then_inc(self.powered[at], 1)

        def deviations(self, act, at):
            act.wait_ge(self.powered[at], self.powered.done(at))
            nc.scalar.activation(self.deviation[:, at.k], self.power[:, at.k], ACT.Sqrt, bias=eps[:, 0:1],
                                 scale=1.0 / D).then_inc(self.rooted[at], 1)

        def invert(self, dve, at):
            dve.wait_ge(self.rooted[at], self.rooted.done(at))
            nc.vector.reciprocal(self.scale[:, at.k], self.deviation[:, at.k]).then_inc(self.scaled[at], 1)

        def scale_rows(self, dve, at, stored):
            dve.wait_ge(self.scaled[at], self.scaled.done(at))
            if (at - DEEP).exists:
                dve.wait_ge(stored[at - DEEP], stored.done(at - DEEP))
            nc.vector.tensor_tensor(self.out[:, at.k], self.centred[:, at.k], of_row(self.scale[:, at.k]),
                                    ALU.mult).then_inc(self.ready[at], 1)

    def scale_phase():
        with ExitStack() as c:
            xt = sb(c, "sc_x", [P, DEEP, ROWS, D])
            yt = sb(c, "sc_y", [P, DEEP, ROWS, D])
            loaded, stored = sig.landing("nodes_loaded", 16), sig.landing("nodes_stored", 16)
            ready = sig.get("node_result")
            with nc.Block() as block:
                @block.sync
                def _(sp):
                    def load(at):
                        if (at - DEEP).exists:
                            sp.wait_ge(ready[at - DEEP], ready.done(at - DEEP))
                        load_nodes(sp, at, [(x, xt[:, at.k])], loaded)

                    def store(at):
                        store_nodes(sp, at, y_table, yt[:, at.k], ready, stored)
                    over_blocks(sp, (load, 0), (store, 3))
                    wait_stored(sp, stored)

                @block.vector
                def _(dve):
                    def scale(at):
                        dve.wait_ge(loaded[at], loaded.done(at))
                        if (at - DEEP).exists:
                            dve.wait_ge(stored[at - DEEP], stored.done(at - DEEP))
                        nc.vector.tensor_tensor(yt[:, at.k], xt[:, at.k], dinv_of(at), ALU.mult).then_inc(ready[at], 1)
                    over_blocks(dve, (scale, 0))
            sig.end_phase()

    def edge_flags(at, parts):
        return same_flags[bass.ds(at.times(EDGE_BLOCK), EDGE_BLOCK)].partition_broadcast(parts)

    def edge_features(attr, at, to):
        if at.is_last:
            first = (BLOCKS - 1) * EDGE_BLOCK
            full = (EDGES - first) // P
            rest = EDGES - first - full * P
            return [(to(slice(0, P), slice(0, full)), attr[first:first + full * P, :].rearrange("(t p) d -> p t d", p=P)),
                    (to(slice(0, rest), full), attr[first + full * P:EDGES, :])]
        whole = attr[bass.ds(at.times(EDGE_BLOCK), EDGE_BLOCK), :].rearrange("(t p) d -> p t d", p=P)
        return [(to(slice(0, P), slice(0, 2)), whole[:, 0:2, :]), (to(slice(0, P), slice(2, 4)), whole[:, 2:4, :])]

    class Rows:

        def __init__(self, c, source, sides):
            self.source, self.sides = source, sides
            self.rows = sb(c, "edge_rows", [P, DEEP, TILES, sides * D])
            self.idx = sb(c, "edge_idx", [P, 2, DEEP, TILES], I32)
            self.put = sb(c, "edge_put", [P, DEEP, TILES], I32)
            self.back = sb(c, "edge_back", [P, DEEP, TILES, D])
            self.index_staged, self.put_staged = sig.get("index_staged"), sig.get("put_staged")
            self.gathered = sig.landing("gathered", 16 * TILES * sides)
            self.scattered = sig.landing("scattered", 16 * TILES)
            self.turned, self.staged = sig.get("rows_turned"), sig.get("staged")

        def stage_index(self, pool, at):
            if at.k % 2:
                return
            if (at - DEEP).exists:
                pool.wait_ge(self.gathered[at - DEEP], self.gathered.done(at - DEEP))
                pool.sem_inc(pool_passed, 1)
                pool.wait_ge(self.gathered[at - (DEEP - 1)], self.gathered.done(at - (DEEP - 1)))
                pool.sem_inc(pool_passed, 1)
            nc.gpsimd.tensor_copy(self.idx[:, 0:self.sides, at.k:at.k + 2, :].rearrange("p s k t -> p s (k t)"),
                                  edge_idx[:, 0:self.sides, bass.ds(at.times(TILES), 2 * TILES)]).then_inc(self.index_staged[at], 2)

        def gather(self, pool, at):
            pool.wait_ge(self.index_staged[at], self.index_staged.done(at))
            if (at - DEEP).exists:
                pool.wait_ge(self.turned[at - DEEP], self.turned.done(at - DEEP))
            pool.sem_inc(pool_passed, 1)
            for t in range(TILES):
                for side in range(self.sides):
                    nc.gpsimd.indirect_dma_start(
                        out=self.rows[:, at.k, t, side * D:(side + 1) * D], out_offset=None, in_=self.source,
                        in_offset=bass.IndirectOffsetOnAxis(ap=self.idx[:, side, at.k, t:t + 1], axis=0)
                    ).then_inc(self.gathered[at], 16)

        def stage_put(self, pool, at):
            if at.k % 2:
                return
            if (at - DEEP).exists:
                pool.wait_ge(self.scattered[at - DEEP], self.scattered.done(at - DEEP))
                pool.sem_inc(pool_passed, 1)
                pool.wait_ge(self.scattered[at - (DEEP - 1)], self.scattered.done(at - (DEEP - 1)))
                pool.sem_inc(pool_passed, 1)
            nc.gpsimd.tensor_copy(self.put[:, at.k:at.k + 2, :].rearrange("p k t -> p (k t)"),
                                  put_idx[:, bass.ds(at.times(TILES), 2 * TILES)]).then_inc(self.put_staged[at], 2)

        def scatter(self, pool, at):
            pool.wait_ge(self.put_staged[at], self.put_staged.done(at))
            pool.wait_ge(self.staged[at], self.staged.done(at))
            pool.sem_inc(pool_passed, 1)
            for t in range(TILES):
                nc.gpsimd.indirect_dma_start(
                    out=sums, out_offset=bass.IndirectOffsetOnAxis(ap=self.put[:, at.k, t:t + 1], axis=0),
                    in_=self.back[:, at.k, t, :], in_offset=None, bounds_check=NODES - 1,
                    oob_is_err=False).then_inc(self.scattered[at], 16)

        def run(self, pool, lag):
            def stage_index(at):
                self.stage_index(pool, at)

            def gather(at):
                self.gather(pool, at)

            def stage_put(at):
                self.stage_put(pool, at)

            def scatter(at):
                self.scatter(pool, at)
            over_blocks(pool, (stage_index, 0), (stage_put, lag), (gather, 1), (scatter, lag + 1))
            for at in last_blocks():
                pool.wait_ge(self.scattered[at], self.scattered.done(at))

    def sum_phase(source):
        with ExitStack() as c:
            io = Rows(c, source, 1)
            same = sb(c, "es_same", [D, DEEP, EDGE_BLOCK], BF16)
            scan = sb(c, "es_scan", [D, 2, EDGE_BLOCK])
            start = sb(c, "es_start", [D, 1])
            rows_t = [pb(c, f"es_rows_t{h}", [D, EDGE_BLOCK]) for h in range(2)]
            back_t = [pb(c, f"es_back_t{h}", [P, TILES, D]) for h in range(2)]
            loaded = sig.landing("edges_loaded", 16)
            gathered, turned, staged, scattered = io.gathered, io.turned, io.staged, io.scattered
            scanned, turned_back = sig.get("scanned"), sig.get("turned_back")
            start_set = sem(f"start_set_{source.name}")
            with nc.Block() as block:
                @block.sync
                def _(sp):
                    def load(at):
                        if (at - DEEP).exists:
                            sp.wait_ge(scanned[at - DEEP], scanned.done(at - DEEP))
                        sp.sem_inc(sp_passed, 1)
                        sp.dma_start(same[:, at.k, :], edge_flags(at, D)).then_inc(loaded[at], 16)
                    over_blocks(sp, (load, 0))

                @block.gpsimd
                def _(pool):
                    io.run(pool, 3)

                @block.tensor
                def _(pe):
                    def turn(at):
                        pe.wait_ge(gathered[at], gathered.done(at))
                        if (at - 2).exists:
                            pe.wait_ge(scanned[at - 2], scanned.done(at - 2))
                        pe.sem_inc(pe_passed, 1)
                        for t in range(TILES):
                            last = nc.tensor.transpose(rows_t[at.h][:, t * P:(t + 1) * P], io.rows[:, at.k, t, :], ident[:, :])
                        last.then_inc(turned[at], 1)

                    def turn_back(at):
                        pe.wait_ge(scanned[at], scanned.done(at))
                        if (at - 2).exists:
                            pe.wait_ge(staged[at - 2], staged.done(at - 2))
                        pe.sem_inc(pe_passed, 1)
                        for t in range(TILES):
                            last = nc.tensor.transpose(back_t[at.h][:, t, :], scan[:, at.h, t * P:(t + 1) * P], ident[0:D, 0:D])
                        last.then_inc(turned_back[at], 1)
                    over_blocks(pe, (turn, 0), (turn_back, 1))

                @block.vector
                def _(dve):
                    nc.vector.memset(start[:, :], 0.0).then_inc(start_set, 1)
                    dve.wait_ge(start_set, 1)

                    def sum_up(at):
                        dve.wait_ge(turned[at], turned.done(at))
                        dve.wait_ge(loaded[at], loaded.done(at))
                        if (at - 2).exists:
                            dve.wait_ge(turned_back[at - 2], turned_back.done(at - 2))
                        carry = start[:, 0:1]
                        if (at - 1).exists:
                            dve.wait_ge(scanned[at - 1], scanned.done(at - 1))
                            carry = scan[:, 1 - at.h, EDGE_BLOCK - 1:EDGE_BLOCK]
                        nc.vector.tensor_tensor_scan(scan[:, at.h, :], same[:, at.k, :], rows_t[at.h][:, :], carry,
                                                     ALU.mult, ALU.add).then_inc(scanned[at], 1)
                    over_blocks(dve, (sum_up, 0))

                @block.scalar
                def _(act):
                    def stage(at):
                        act.wait_ge(turned_back[at], turned_back.done(at))
                        if (at - DEEP).exists:
                            act.wait_ge(scattered[at - DEEP], scattered.done(at - DEEP))
                        nc.scalar.activation(io.back[:, at.k], back_t[at.h][:, :, :], ACT.Copy).then_inc(staged[at], 1)
                    over_blocks(act, (stage, 1))
            sig.end_phase()

    def attention_phase(source, relations):
        with ExitStack() as c:
            io = Rows(c, source, 2)
            same = sb(c, "ea_same", [P, DEEP, EDGE_BLOCK], BF16)
            low = sb(c, "ea_low", [P, 2, EDGE_BLOCK], BF16)
            rows_s = sb(c, "ea_rows_s", [P, DEEP, EDGE_BLOCK])
            peak = sb(c, "ea_peak", [P, 2, EDGE_BLOCK + 1])
            fall = sb(c, "ea_fall", [P, 2, EDGE_BLOCK])
            fell = sb(c, "ea_fell", [P, 2, EDGE_BLOCK])
            below = sb(c, "ea_below", [P, 2, EDGE_BLOCK])
            decay = sb(c, "ea_decay", [P, 2, EDGE_BLOCK])
            weight = sb(c, "ea_weight", [D, 2, EDGE_BLOCK])
            terms = sb(c, "ea_terms", [P, 2, EDGE_BLOCK])
            scan = sb(c, "ea_scan", [P, 2, EDGE_BLOCK])
            guard = sb(c, "ea_guard", [P, 2, TILES])
            share = sb(c, "ea_share", [P, 2, TILES])
            start = sb(c, "ea_start", [P, 2])
            rows_t = [pb(c, f"ea_rows_t{h}", [P, EDGE_BLOCK]) for h in range(2)]
            proj_t = [pb(c, f"ea_proj_t{h}", [P, EDGE_BLOCK]) for h in range(2)]
            score_t = [pb(c, f"ea_score_t{h}", [P, EDGE_BLOCK]) for h in range(2)]
            back_t = [pb(c, f"ea_back_t{h}", [P, TILES, P]) for h in range(2)]
            loaded = sig.landing("edges_loaded", 16 * (4 if relations else 1))
            gathered, turned, staged, scattered = io.gathered, io.turned, io.staged, io.scattered
            copied = sig.get("rows_copied")
            projected = sig.get("projected", RELS if relations else 1)
            scored, lowered, peaked, peak_kept = sig.get("scored"), sig.get("lowered"), sig.get("peaked"), sig.get("peak_kept")
            falls, fallen, belows = sig.get("falls"), sig.get("fallen"), sig.get("belows")
            decayed, weighed, termed = sig.get("decayed"), sig.get("weighed", 2), sig.get("termed")
            scanned, turned_back = sig.get("scanned"), sig.get("turned_back")
            guarded, shared, activated = sig.get("guarded"), sig.get("shared"), sig.get("activated")
            start_set = sem(f"start_set_{source.name}")
            if relations:
                masked = sb(c, "ea_masked", [P, RELS, EDGE_BLOCK])
                kind = sb(c, "ea_kind", [P, 2, EDGE_BLOCK], I32)
                feats = sb(c, "ea_feats", [P, 2, TILES, P])
                bent = sb(c, "ea_bent", [D, 2, EDGE_BLOCK])
                pair = sb(c, "ea_pair", [D, 2, EDGE_BLOCK])
                masks_made, paired = sig.get("masks_made", RELS), sig.get("paired")
                zeros_set = sem("feature_zeros_set")
                value = rows_s
            else:
                score_s = sb(c, "ea_score_s", [P, 2, EDGE_BLOCK])
                value = sb(c, "ea_value", [P, DEEP, EDGE_BLOCK])
                valued = sig.get("valued")
            with nc.Block() as block:
                @block.sync
                def _(sp):
                    if relations:
                        sp.wait_ge(zeros_set, 1)

                    def load(at):
                        if (at - DEEP).exists:
                            sp.wait_ge(lowered[at - DEEP], lowered.done(at - DEEP))
                            sp.sem_inc(sp_passed, 1)
                        sp.dma_start(same[:, at.k, :], edge_flags(at, P)).then_inc(loaded[at], 16)
                        if not relations:
                            return
                        if (at - 2).exists:
                            sp.wait_ge(masks_made[at - 2], masks_made.done(at - 2))
                            sp.sem_inc(sp_passed, 1)
                            sp.wait_ge(projected[at - 2], projected.done(at - 2))
                            sp.sem_inc(sp_passed, 1)
                        moves = edge_features(ins["edge_attr_64"], at, lambda p, t: feats[p, at.h, t, D:P])
                        types = ins["edge_type_10"]
                        if at.is_last:
                            left = EDGES - (BLOCKS - 1) * EDGE_BLOCK
                            moves.append((kind[:, at.h, 0:left], types[EDGES - left:EDGES].partition_broadcast(P)))
                        else:
                            moves.append((kind[:, at.h, :],
                                          types[bass.ds(at.times(EDGE_BLOCK), EDGE_BLOCK)].partition_broadcast(P)))
                        for to, of in moves:
                            sp.dma_start(to, of).then_inc(loaded[at], 16)
                    over_blocks(sp, (load, 0))

                @block.gpsimd
                def _(pool):
                    io.run(pool, 5 if relations else 4)

                @block.tensor
                def _(pe):
                    def turn(at):
                        pe.wait_ge(gathered[at], gathered.done(at))
                        if (at - 2).exists:
                            pe.wait_ge(copied[at - 2], copied.done(at - 2))
                        pe.sem_inc(pe_passed, 1)
                        for t in range(TILES):
                            last = nc.tensor.transpose(rows_t[at.h][:, t * P:(t + 1) * P], io.rows[:, at.k, t, :], ident[:, :])
                        last.then_inc(turned[at], 1)

                    def project_relations(at):
                        pe.wait_ge(loaded[at], loaded.done(at))
                        if (at - 2).exists:
                            pe.wait_ge(paired[at - 2], paired.done(at - 2))
                        for t in range(TILES):
                            nc.tensor.matmul(proj_t[at.h][:, t * P:(t + 1) * P], feats[:, at.h, t, :], ident[:, :],
                                             start=(t == 0), stop=False, skip_group_check=True)
                        for r in range(RELS):
                            pe.wait_ge(masks_made[at], masks_made.part(at, r + 1))
                            nc.tensor.matmul(proj_t[at.h][:, :], rel2[:, r, :], masked[:, r, :], start=False,
                                             stop=(r == RELS - 1), skip_group_check=True).then_inc(projected[at], 1)

                    def project(at):
                        pe.wait_ge(copied[at], copied.done(at))
                        if (at - 2).exists:
                            pe.wait_ge(valued[at - 2], valued.done(at - 2))
                        nc.tensor.matmul(proj_t[at.h][:, :], w_out2[:, :], rows_s[:, at.k, :], start=True,
                                         stop=True).then_inc(projected[at], 1)

                    def score_relations(at):
                        pe.wait_ge(paired[at], paired.done(at))
                        if (at - 2).exists:
                            pe.wait_ge(belows[at - 2], belows.done(at - 2))
                        nc.tensor.matmul(score_t[at.h][:, :], ones[0:D, :], pair[:, at.h, :], start=True,
                                         stop=True).then_inc(scored[at], 1)

                    def score(at):
                        pe.wait_ge(valued[at], valued.done(at))
                        if (at - 2).exists:
                            pe.wait_ge(activated[at - 2], activated.done(at - 2))
                        nc.tensor.matmul(score_t[at.h][:, :], attn_all[:, :], value[:, at.k, :], start=True,
                                         stop=True).then_inc(scored[at], 1)

                    def turn_back(at):
                        pe.wait_ge(scanned[at], scanned.done(at))
                        if (at - 2).exists:
                            pe.wait_ge(staged[at - 2], staged.done(at - 2))
                        pe.sem_inc(pe_passed, 1)
                        for t in range(TILES):
                            last = nc.tensor.transpose(back_t[at.h][:, t, :], scan[:, at.h, t * P:(t + 1) * P], ident[:, :])
                        last.then_inc(turned_back[at], 1)
                    if relations:
                        over_blocks(pe, (turn, 0), (turn_back, 4), (score_relations, 2), (project_relations, 1))
                    else:
                        over_blocks(pe, (turn_back, 3), (project, 1), (turn, 0), (score, 1))

                @block.scalar
                def _(act):
                    def copy_rows(at):
                        act.wait_ge(turned[at], turned.done(at))
                        if (at - DEEP).exists:
                            if relations:
                                act.wait_ge(masks_made[at - DEEP], masks_made.done(at - DEEP))
                                act.wait_ge(termed[at - DEEP], termed.done(at - DEEP))
                            else:
                                act.wait_ge(projected[at - DEEP], projected.done(at - DEEP))
                        nc.scalar.activation(rows_s[:, at.k, :], rows_t[at.h][:, :], ACT.Copy).then_inc(copied[at], 1)

                    def bend(at):
                        act.wait_ge(projected[at], projected.done(at))
                        if (at - 2).exists:
                            act.wait_ge(paired[at - 2], paired.done(at - 2))
                        nc.scalar.activation(bent[:, at.h, :], proj_t[at.h][D:P, :], ACT.Tanh).then_inc(activated[at], 1)

                    def add_bias(at):
                        act.wait_ge(projected[at], projected.done(at))
                        if (at - DEEP).exists:
                            act.wait_ge(termed[at - DEEP], termed.done(at - DEEP))
                        nc.scalar.activation(value[:, at.k, :], proj_t[at.h][:, :], ACT.Identity,
                                             bias=b_out2[:, 0:1]).then_inc(valued[at], 1)

                    def gelu(at):
                        act.wait_ge(scored[at], scored.done(at))
                        if (at - 2).exists:
                            act.wait_ge(belows[at - 2], belows.done(at - 2))
                        nc.scalar.activation(score_s[:, at.h, :], score_t[at.h][:, :], ACT.Gelu).then_inc(activated[at], 1)

                    def weigh(at):
                        act.wait_ge(fallen[at], fallen.done(at))
                        if (at - 2).exists:
                            act.wait_ge(scanned[at - 2], scanned.done(at - 2))
                        nc.scalar.activation(decay[:, at.h, :], fell[:, at.h, :], ACT.Exp).then_inc(decayed[at], 1)
                        act.wait_ge(belows[at], belows.done(at))
                        if (at - 2).exists:
                            act.wait_ge(termed[at - 2], termed.done(at - 2))
                        nc.scalar.activation(weight[:, at.h, :], below[0:D, at.h, :], ACT.Exp).then_inc(weighed[at], 1)
                        nc.scalar.activation(terms[D:P, at.h, :], below[D:P, at.h, :], ACT.Exp).then_inc(weighed[at], 1)
                    if relations:
                        over_blocks(act, (bend, 2), (weigh, 3), (copy_rows, 0))
                    else:
                        over_blocks(act, (weigh, 2), (add_bias, 1), (copy_rows, 0), (gelu, 1))

                @block.vector
                def _(dve):
                    nc.vector.memset(start[:, 0:1], LOW).then_inc(start_set, 1)
                    nc.vector.memset(start[:, 1:2], 0.0).then_inc(start_set, 1)
                    if relations:
                        nc.vector.memset(feats[:, :, :, :], 0.0).then_inc(zeros_set, 1)
                    dve.wait_ge(start_set, 2)

                    def mask(at):
                        dve.wait_ge(copied[at], copied.done(at))
                        dve.wait_ge(loaded[at], loaded.done(at))
                        for r in range(RELS):
                            if (at - 1).exists:
                                dve.wait_ge(projected[at - 1], projected.part(at - 1, r + 1))
                            nc.vector.scalar_tensor_tensor(out=masked[:, r, :], in0=kind[:, at.h, :], scalar=float(r),
                                                           in1=rows_s[:, at.k, :], op0=ALU.is_equal,
                                                           op1=ALU.mult).then_inc(masks_made[at], 1)

                    def pair_up(at):
                        dve.wait_ge(activated[at], activated.done(at))
                        if (at - 2).exists:
                            dve.wait_ge(scored[at - 2], scored.done(at - 2))
                        nc.vector.tensor_tensor(pair[:, at.h, :], proj_t[at.h][0:D, :], bent[:, at.h, :],
                                                ALU.mult).then_inc(paired[at], 1)

                    def carry_peak(at):
                        dve.wait_ge(loaded[at], loaded.done(at))
                        if (at - 2).exists:
                            dve.wait_ge(falls[at - 2], falls.done(at - 2))
                        nc.vector.tensor_scalar(low[:, at.h, :], same[:, at.k, :], -1.0, -LOW, ALU.add,
                                                ALU.mult).then_inc(lowered[at], 1)
                        carried = start[:, 0:1]
                        if (at - 1).exists:
                            dve.wait_ge(peaked[at - 1], peaked.done(at - 1))
                            carried = peak[:, 1 - at.h, EDGE_BLOCK:EDGE_BLOCK + 1]
                        if (at - 2).exists:
                            dve.wait_ge(fallen[at - 2], fallen.done(at - 2))
                            dve.wait_ge(belows[at - 2], belows.done(at - 2))
                            dve.wait_ge(peak_kept[at - 1], peak_kept.done(at - 1))
                        nc.vector.tensor_copy(peak[:, at.h, 0:1], carried).then_inc(peak_kept[at], 1)

                    def scores_of(at):
                        return score_t[at.h][:, :] if relations else score_s[:, at.h, :]

                    def raise_peak(at):
                        if relations:
                            dve.wait_ge(scored[at], scored.done(at))
                        else:
                            dve.wait_ge(activated[at], activated.done(at))
                        dve.wait_ge(lowered[at], lowered.done(at))
                        dve.wait_ge(peak_kept[at], peak_kept.done(at))
                        nc.vector.tensor_tensor_scan(peak[:, at.h, 1:EDGE_BLOCK + 1], low[:, at.h, :], scores_of(at),
                                                     peak[:, at.h, 0:1], ALU.add, ALU.max).then_inc(peaked[at], 1)

                    def soften(at):
                        dve.wait_ge(peaked[at], peaked.done(at))
                        nc.vector.tensor_tensor(fall[:, at.h, :], peak[:, at.h, 0:EDGE_BLOCK], low[:, at.h, :],
                                                ALU.add).then_inc(falls[at], 1)
                        if (at - 2).exists:
                            dve.wait_ge(weighed[at - 2], weighed.done(at - 2))
                        nc.vector.tensor_tensor(below[:, at.h, :], scores_of(at), peak[:, at.h, 1:EDGE_BLOCK + 1],
                                                ALU.subtract).then_inc(belows[at], 1)
                        dve.wait_ge(falls[at], falls.done(at))
                        if (at - 2).exists:
                            dve.wait_ge(decayed[at - 2], decayed.done(at - 2))
                        nc.vector.tensor_tensor(fell[:, at.h, :], fall[:, at.h, :], peak[:, at.h, 1:EDGE_BLOCK + 1],
                                                ALU.subtract).then_inc(fallen[at], 1)

                    def weigh_values(at):
                        dve.wait_ge(weighed[at], weighed.done(at))
                        dve.wait_ge(decayed[at], decayed.done(at))
                        if (at - 2).exists:
                            dve.wait_ge(scanned[at - 2], scanned.done(at - 2))
                        nc.vector.tensor_tensor(terms[0:D, at.h, :], weight[:, at.h, :], value[0:D, at.k, :],
                                                ALU.mult).then_inc(termed[at], 1)

                    def sum_up(at):
                        dve.wait_ge(termed[at], termed.done(at))
                        carried = start[:, 1:2]
                        if (at - 1).exists:
                            dve.wait_ge(scanned[at - 1], scanned.done(at - 1))
                            carried = scan[:, 1 - at.h, EDGE_BLOCK - 1:EDGE_BLOCK]
                        if (at - 2).exists:
                            dve.wait_ge(turned_back[at - 2], turned_back.done(at - 2))
                        nc.vector.tensor_tensor_scan(scan[:, at.h, :], decay[:, at.h, :], terms[:, at.h, :], carried,
                                                     ALU.mult, ALU.add).then_inc(scanned[at], 1)

                    def guard_sums(at):
                        dve.wait_ge(turned_back[at], turned_back.done(at))
                        if (at - 2).exists:
                            dve.wait_ge(shared[at - 2], shared.done(at - 2))
                        nc.vector.tensor_scalar(guard[:, at.h, :], back_t[at.h][:, :, D], 1e-20, None,
                                                ALU.max).then_inc(guarded[at], 1)

                    def invert_sums(at):
                        dve.wait_ge(guarded[at], guarded.done(at))
                        if (at - 2).exists:
                            dve.wait_ge(staged[at - 2], staged.done(at - 2))
                        nc.vector.reciprocal(share[:, at.h, :], guard[:, at.h, :]).then_inc(shared[at], 1)

                    def share_out(at):
                        dve.wait_ge(shared[at], shared.done(at))
                        if (at - DEEP).exists:
                            dve.wait_ge(scattered[at - DEEP], scattered.done(at - DEEP))
                        nc.vector.tensor_tensor(io.back[:, at.k], back_t[at.h][:, :, 0:D],
                                                share[:, at.h, :].unsqueeze(2).to_broadcast([P, TILES, D]),
                                                ALU.mult).then_inc(staged[at], 1)
                    if relations:
                        over_blocks(dve, (pair_up, 2), (carry_peak, 2), (mask, 1), (guard_sums, 4), (raise_peak, 2),
                                    (invert_sums, 4), (weigh_values, 3), (soften, 2), (sum_up, 3), (share_out, 4))
                    else:
                        over_blocks(dve, (weigh_values, 2), (carry_peak, 1), (sum_up, 2), (guard_sums, 3), (raise_peak, 1),
                                    (invert_sums, 3), (soften, 1), (share_out, 3))
            sig.end_phase()

    def message_phase(source):
        with ExitStack() as c:
            io = Rows(c, source, 2)
            same = sb(c, "em_same", [D, DEEP, EDGE_BLOCK], BF16)
            feats = sb(c, "em_feats", [P, DEEP, TILES, DE])
            rows_s = sb(c, "em_rows_s", [P, 2, EDGE_BLOCK])
            feats_s = sb(c, "em_feats_s", [DE, 2, EDGE_BLOCK])
            hidden = sb(c, "em_hidden", [HID, 2, EDGE_BLOCK])
            message = sb(c, "em_message", [D, 2, EDGE_BLOCK])
            scan = sb(c, "em_scan", [D, 2, EDGE_BLOCK])
            start = sb(c, "em_start", [D, 1])
            rows_t = [pb(c, f"em_rows_t{h}", [P, EDGE_BLOCK]) for h in range(2)]
            feats_t = pb(c, "em_feats_t", [DE, EDGE_BLOCK])
            hidden_t = [pb(c, f"em_hidden_t{h}", [HID, EDGE_BLOCK]) for h in range(2)]
            message_t = pb(c, "em_message_t", [D, EDGE_BLOCK])
            back_t = [pb(c, f"em_back_t{h}", [P, TILES, D]) for h in range(2)]
            loaded = sig.landing("edges_loaded", 16 * 3)
            gathered, turned, staged, scattered = io.gathered, io.turned, io.staged, io.scattered
            feats_copied, copied = sig.get("feats_copied"), sig.get("rows_copied")
            projected, activated = sig.get("projected"), sig.get("activated")
            scored, valued = sig.get("scored"), sig.get("valued")
            scanned, turned_back = sig.get("scanned"), sig.get("turned_back")
            start_set = sem("start_set_messages")
            with nc.Block() as block:
                @block.sync
                def _(sp):
                    def load(at):
                        if (at - DEEP).exists:
                            sp.wait_ge(scanned[at - DEEP], scanned.done(at - DEEP))
                            sp.sem_inc(sp_passed, 1)
                            sp.wait_ge(turned[at - DEEP], turned.done(at - DEEP))
                            sp.sem_inc(sp_passed, 1)
                        sp.dma_start(same[:, at.k, :], edge_flags(at, D)).then_inc(loaded[at], 16)
                        for to, of in edge_features(ins["edge_attr_32"], at, lambda p, t: feats[p, at.k, t, :]):
                            sp.dma_start(to, of).then_inc(loaded[at], 16)
                    over_blocks(sp, (load, 0))

                @block.gpsimd
                def _(pool):
                    io.run(pool, DEEP)

                @block.tensor
                def _(pe):
                    def turn(at):
                        pe.wait_ge(loaded[at], loaded.done(at))
                        if (at - 1).exists:
                            pe.wait_ge(feats_copied[at - 1], feats_copied.done(at - 1))
                        pe.sem_inc(pe_passed, 1)
                        for t in range(TILES):
                            nc.tensor.transpose(feats_t[:, t * P:(t + 1) * P], feats[:, at.k, t, :], ident[:, :])
                        pe.wait_ge(gathered[at], gathered.done(at))
                        if (at - 2).exists:
                            pe.wait_ge(copied[at - 2], copied.done(at - 2))
                        pe.sem_inc(pe_passed, 1)
                        for t in range(TILES):
                            last = nc.tensor.transpose(rows_t[at.h][:, t * P:(t + 1) * P], io.rows[:, at.k, t, :], ident[:, :])
                        last.then_inc(turned[at], 1)

                    def hide(at):
                        pe.wait_ge(copied[at], copied.done(at))
                        pe.wait_ge(feats_copied[at], feats_copied.done(at))
                        if (at - 2).exists:
                            pe.wait_ge(activated[at - 2], activated.done(at - 2))
                        nc.tensor.matmul(hidden_t[at.h][:, :], m_w1[:, :], rows_s[:, at.h, :], start=True, stop=False)
                        nc.tensor.matmul(hidden_t[at.h][:, :], m_w1e[:, :], feats_s[:, at.h, :], start=False,
                                         stop=True).then_inc(projected[at], 1)

                    def write(at):
                        pe.wait_ge(activated[at], activated.done(at))
                        if (at - 1).exists:
                            pe.wait_ge(valued[at - 1], valued.done(at - 1))
                        nc.tensor.matmul(message_t[:, :], m_w2[:, :], hidden[:, at.h, :], start=True, stop=True).then_inc(scored[at], 1)

                    def turn_back(at):
                        pe.wait_ge(scanned[at], scanned.done(at))
                        if (at - 2).exists:
                            pe.wait_ge(staged[at - 2], staged.done(at - 2))
                        pe.sem_inc(pe_passed, 1)
                        for t in range(TILES):
                            last = nc.tensor.transpose(back_t[at.h][:, t, :], scan[:, at.h, t * P:(t + 1) * P], ident[0:D, 0:D])
                        last.then_inc(turned_back[at], 1)
                    over_blocks(pe, (turn_back, 3), (write, 2), (hide, 1), (turn, 0))

                @block.scalar
                def _(act):
                    def copy_rows(at):
                        act.wait_ge(turned[at], turned.done(at))
                        if (at - 2).exists:
                            act.wait_ge(projected[at - 2], projected.done(at - 2))
                        nc.scalar.activation(feats_s[:, at.h, :], feats_t[:, :], ACT.Copy).then_inc(feats_copied[at], 1)
                        nc.scalar.activation(rows_s[:, at.h, :], rows_t[at.h][:, :], ACT.Copy).then_inc(copied[at], 1)

                    def rectify(at):
                        act.wait_ge(projected[at], projected.done(at))
                        if (at - 2).exists:
                            act.wait_ge(scored[at - 2], scored.done(at - 2))
                        nc.scalar.activation(hidden[:, at.h, :], hidden_t[at.h][:, :], ACT.Relu, bias=m_b1[:, 0:1]).then_inc(activated[at], 1)

                    def add_bias(at):
                        act.wait_ge(scored[at], scored.done(at))
                        if (at - 2).exists:
                            act.wait_ge(scanned[at - 2], scanned.done(at - 2))
                        nc.scalar.activation(message[:, at.h, :], message_t[:, :], ACT.Identity, bias=m_b2[:, 0:1]).then_inc(valued[at], 1)
                    over_blocks(act, (add_bias, 2), (rectify, 1), (copy_rows, 0))

                @block.vector
                def _(dve):
                    nc.vector.memset(start[:, :], 0.0).then_inc(start_set, 1)
                    dve.wait_ge(start_set, 1)

                    def sum_up(at):
                        dve.wait_ge(valued[at], valued.done(at))
                        dve.wait_ge(loaded[at], loaded.done(at))
                        if (at - 2).exists:
                            dve.wait_ge(turned_back[at - 2], turned_back.done(at - 2))
                        carried = start[:, 0:1]
                        if (at - 1).exists:
                            dve.wait_ge(scanned[at - 1], scanned.done(at - 1))
                            carried = scan[:, 1 - at.h, EDGE_BLOCK - 1:EDGE_BLOCK]
                        nc.vector.tensor_tensor_scan(scan[:, at.h, :], same[:, at.k, :], message[:, at.h, :], carried,
                                                     ALU.mult, ALU.add).then_inc(scanned[at], 1)

                    def stage(at):
                        dve.wait_ge(turned_back[at], turned_back.done(at))
                        if (at - DEEP).exists:
                            dve.wait_ge(scattered[at - DEEP], scattered.done(at - DEEP))
                        nc.vector.tensor_copy(io.back[:, at.k], back_t[at.h][:, :, :]).then_inc(staged[at], 1)
                    over_blocks(dve, (stage, 3), (sum_up, 2))
            sig.end_phase()

    def gcn_phase():
        with ExitStack() as c:
            agg = sb(c, "ng_agg", [P, DEEP, ROWS, D])
            own = sb(c, "ng_own", [P, DEEP, ROWS, D])
            both = sb(c, "ng_both", [P, 2, ROWS, D])
            unit = sb(c, "ng_unit", [P, 2, ROWS, D])
            unit_s = sb(c, "ng_unit_s", [P, 2, 512])
            hidden = sb(c, "ng_hidden", [HID, 2, 2, 512])
            res = sb(c, "ng_res", [P, DEEP, ROWS, D])
            unit_t = [pb(c, f"ng_unit_t{h}", [P, 512]) for h in range(2)]
            hidden_t = [pb(c, f"ng_hidden_t{h}", [HID, 2, 512]) for h in range(2)]
            out_s = sb(c, "ng_out_s", [P, 2, 512])
            out_t = pb(c, "ng_out_t", [P, 512])
            back_t = pb(c, "ng_back_t", [P, ROWS, D])
            loaded, stored = sig.landing("nodes_loaded", 32), sig.landing("nodes_stored", 16)
            added, united = sig.get("node_added"), sig.get("node_united")
            turned, copied = sig.get("rows_turned"), sig.get("rows_copied")
            projected, activated, scored = sig.get("projected"), sig.get("activated"), sig.get("scored")
            out_copied, turned_back, ready = sig.get("staged"), sig.get("turned_back"), sig.get("node_result")
            with nc.Block() as block:
                @block.sync
                def _(sp):
                    def load(at):
                        if (at - DEEP).exists:
                            sp.wait_ge(added[at - DEEP], added.done(at - DEEP))
                        load_nodes(sp, at, [(sums, agg[:, at.k]), (y_table, own[:, at.k])], loaded)

                    def store(at):
                        store_nodes(sp, at, h_table, res[:, at.k], ready, stored)
                    over_blocks(sp, (load, 0), (store, 8))
                    wait_stored(sp, stored)

                @block.gpsimd
                def _(pool):
                    def add(at):
                        pool.wait_ge(loaded[at], loaded.done(at))
                        if (at - 2).exists:
                            pool.wait_ge(united[at - 2], united.done(at - 2))
                        nc.gpsimd.tensor_tensor(both[:, at.h], agg[:, at.k], own[:, at.k], ALU.add).then_inc(added[at], 1)
                    over_blocks(pool, (add, 0))

                @block.vector
                def _(dve):
                    def unite(at):
                        dve.wait_ge(added[at], added.done(at))
                        if (at - 2).exists:
                            dve.wait_ge(turned[at - 2], turned.done(at - 2))
                        nc.vector.tensor_tensor(unit[:, at.h], both[:, at.h], dinv_of(at), ALU.mult).then_inc(united[at], 1)

                    def finish(at):
                        dve.wait_ge(turned_back[at], turned_back.done(at))
                        if (at - DEEP).exists:
                            dve.wait_ge(stored[at - DEEP], stored.done(at - DEEP))
                        nc.vector.tensor_tensor(res[:, at.k], back_t[:, :, :], dinv_of(at), ALU.mult).then_inc(ready[at], 1)
                    over_blocks(dve, (finish, 5), (unite, 0))

                @block.tensor
                def _(pe):
                    def turn(at):
                        pe.wait_ge(united[at], united.done(at))
                        if (at - 2).exists:
                            pe.wait_ge(copied[at - 2], copied.done(at - 2))
                        pe.sem_inc(pe_passed, 1)
                        for q in range(ROWS // 2):
                            last = nc.tensor.transpose(unit_t[at.h][:, q * P:(q + 1) * P],
                                                       unit[:, at.h, 2 * q:2 * q + 2, :].rearrange("p j d -> p (j d)"), ident[:, :])
                        last.then_inc(turned[at], 1)

                    def hide(at):
                        pe.wait_ge(copied[at], copied.done(at))
                        if (at - 2).exists:
                            pe.wait_ge(activated[at - 2], activated.done(at - 2))
                        for odd in range(2):
                            k = slice(odd * D, odd * D + D)
                            last = nc.tensor.matmul(hidden_t[at.h][:, odd, :], w1[k, :], unit_s[k, at.h, :], start=True, stop=True)
                        last.then_inc(projected[at], 1)

                    def write(at):
                        pe.wait_ge(activated[at], activated.done(at))
                        if (at - 1).exists:
                            pe.wait_ge(out_copied[at - 1], out_copied.done(at - 1))
                        for odd in range(2):
                            last = nc.tensor.matmul(out_t[:, :], w2_pair[:, odd, :], hidden[:, at.h, odd, :],
                                                    start=(odd == 0), stop=(odd == 1))
                        last.then_inc(scored[at], 1)

                    def turn_back(at):
                        pe.wait_ge(out_copied[at], out_copied.done(at))
                        if (at - 1).exists:
                            pe.wait_ge(ready[at - 1], ready.done(at - 1))
                        pe.sem_inc(pe_passed, 1)
                        for q in range(ROWS // 2):
                            last = nc.tensor.transpose(back_t[:, 2 * q:2 * q + 2, :].rearrange("p j d -> p (j d)"),
                                                       out_s[:, at.h, q * P:(q + 1) * P], ident[:, :])
                        last.then_inc(turned_back[at], 1)
                    over_blocks(pe, (turn, 0), (hide, 1), (turn_back, 3), (write, 2))

                @block.scalar
                def _(act):
                    def copy(at):
                        act.wait_ge(turned[at], turned.done(at))
                        if (at - 2).exists:
                            act.wait_ge(projected[at - 2], projected.done(at - 2))
                        nc.scalar.activation(unit_s[:, at.h, :], unit_t[at.h][:, :], ACT.Copy).then_inc(copied[at], 1)

                    def rectify(at):
                        act.wait_ge(projected[at], projected.done(at))
                        if (at - 2).exists:
                            act.wait_ge(scored[at - 2], scored.done(at - 2))
                        nc.scalar.activation(hidden[:, at.h], hidden_t[at.h][:, :, :], ACT.Relu, bias=b1[:, 0:1]).then_inc(activated[at], 1)

                    def copy_out(at):
                        act.wait_ge(scored[at], scored.done(at))
                        if (at - 2).exists:
                            act.wait_ge(turned_back[at - 2], turned_back.done(at - 2))
                        nc.scalar.activation(out_s[:, at.h, :], out_t[:, :], ACT.Copy).then_inc(out_copied[at], 1)
                    over_blocks(act, (copy, 0), (rectify, 1), (copy_out, 2))
            sig.end_phase()

    def first_norm_phase():
        with ExitStack() as c:
            agg = sb(c, "n1_agg", [P, DEEP, ROWS, D])
            own = sb(c, "n1_own", [P, DEEP, ROWS, D])
            before = sb(c, "n1_before", [P, DEEP, ROWS, D])
            both = sb(c, "n1_both", [P, 2, ROWS, D])
            conv = sb(c, "n1_conv", [P, 2, ROWS, D])
            biased = sb(c, "n1_biased", [P, 2, ROWS, D])
            total = sb(c, "n1_total", [P, 2, ROWS, D])
            loaded, stored = sig.landing("nodes_loaded", 48), sig.landing("nodes_stored", 16)
            added, united, summed = sig.get("node_added"), sig.get("node_united"), sig.get("node_summed")
            with_bias = sig.get("node_biased")
            norm = Norm(c, scalar_sums=True)
            with nc.Block() as block:
                @block.sync
                def _(sp):
                    def load(at):
                        if (at - DEEP).exists:
                            sp.wait_ge(added[at - DEEP], added.done(at - DEEP))
                            sp.sem_inc(sp_passed, 1)
                            sp.wait_ge(with_bias[at - DEEP], with_bias.done(at - DEEP))
                        load_nodes(sp, at, [(sums, agg[:, at.k]), (h_table, own[:, at.k]), (x, before[:, at.k])], loaded)

                    def store(at):
                        store_nodes(sp, at, x1_table, norm.out[:, at.k], norm.ready, stored)
                    over_blocks(sp, (load, 0), (store, 8))
                    wait_stored(sp, stored)

                @block.gpsimd
                def _(pool):
                    def add(at):
                        pool.wait_ge(loaded[at], loaded.done(at))
                        if (at - 2).exists:
                            pool.wait_ge(united[at - 2], united.done(at - 2))
                            pool.wait_ge(summed[at - 2], summed.done(at - 2))
                        nc.gpsimd.tensor_tensor(both[:, at.h], agg[:, at.k], own[:, at.k], ALU.add).then_inc(added[at], 1)
                        nc.gpsimd.tensor_tensor(biased[:, at.h], before[:, at.k], over_rows(b2), ALU.add).then_inc(with_bias[at], 1)
                    over_blocks(pool, (add, 0))

                @block.vector
                def _(dve):
                    def scale(at):
                        dve.wait_ge(added[at], added.done(at))
                        if (at - 2).exists:
                            dve.wait_ge(summed[at - 2], summed.done(at - 2))
                        nc.vector.tensor_tensor(conv[:, at.h], both[:, at.h], dinv_of(at), ALU.mult).then_inc(united[at], 1)

                    def sum_up(at):
                        dve.wait_ge(united[at], united.done(at))
                        dve.wait_ge(with_bias[at], with_bias.done(at))
                        if (at - 2).exists:
                            dve.wait_ge(norm.shifted[at - 2], norm.shifted.done(at - 2))
                        nc.vector.tensor_tensor(total[:, at.h], conv[:, at.h], biased[:, at.h], ALU.add).then_inc(summed[at], 1)

                    def add_up(at):
                        dve.wait_ge(summed[at], summed.done(at))
                        norm.add_up(dve, at, total[:, at.h])

                    def centre(at):
                        norm.centre(dve, at, total[:, at.h])

                    def invert(at):
                        norm.invert(dve, at)

                    def scale_rows(at):
                        norm.scale_rows(dve, at, stored)
                    over_blocks(dve, (invert, 3), (scale, 0), (add_up, 1), (scale_rows, 3), (sum_up, 0), (centre, 1))

                @block.scalar
                def _(act):
                    def squares(at):
                        norm.squares(act, at)

                    def deviations(at):
                        norm.deviations(act, at)
                    over_blocks(act, (deviations, 1), (squares, 0))
            sig.end_phase()

    def attention_norm_phase():
        with ExitStack() as c:
            agg = sb(c, "n2_agg", [P, DEEP, ROWS, D])
            own = sb(c, "n2_own", [P, DEEP, ROWS, D])
            own_s = sb(c, "n2_own_s", [P, 2, 512])
            both = sb(c, "n2_both", [P, 2, ROWS, D])
            biased = sb(c, "n2_biased", [P, DEEP, ROWS, D])
            total = sb(c, "n2_total", [P, 2, ROWS, D])
            own_t = [pb(c, f"n2_own_t{h}", [P, 512]) for h in range(2)]
            out_t = [pb(c, f"n2_out_t{h}", [P, ROWS, D]) for h in range(2)]
            loaded, stored = sig.landing("nodes_loaded", 32), sig.landing("nodes_stored", 16)
            added, summed, with_bias = sig.get("node_added"), sig.get("node_summed"), sig.get("node_biased")
            turned, copied, projected = sig.get("rows_turned"), sig.get("rows_copied"), sig.get("projected")
            norm = Norm(c, scalar_sums=True)
            with nc.Block() as block:
                @block.sync
                def _(sp):
                    def load(at):
                        if (at - DEEP).exists:
                            sp.wait_ge(added[at - DEEP], added.done(at - DEEP))
                            sp.sem_inc(sp_passed, 1)
                            sp.wait_ge(turned[at - DEEP], turned.done(at - DEEP))
                        load_nodes(sp, at, [(sums, agg[:, at.k]), (x1_table, own[:, at.k])], loaded)

                    def store(at):
                        store_nodes(sp, at, x2_table, norm.out[:, at.k], norm.ready, stored)
                    over_blocks(sp, (load, 0), (store, 8))
                    wait_stored(sp, stored)

                @block.gpsimd
                def _(pool):
                    def add(at):
                        pool.wait_ge(loaded[at], loaded.done(at))
                        if (at - 2).exists:
                            pool.wait_ge(with_bias[at - 2], with_bias.done(at - 2))
                        nc.gpsimd.tensor_tensor(both[:, at.h], agg[:, at.k], own[:, at.k], ALU.add).then_inc(added[at], 1)
                        pool.wait_ge(added[at], added.done(at))
                        if (at - DEEP).exists:
                            pool.wait_ge(summed[at - DEEP], summed.done(at - DEEP))
                        nc.gpsimd.tensor_tensor(biased[:, at.k], both[:, at.h], over_rows(res_b), ALU.add).then_inc(with_bias[at], 1)
                    over_blocks(pool, (add, 0))

                @block.tensor
                def _(pe):
                    def turn(at):
                        pe.wait_ge(loaded[at], loaded.done(at))
                        if (at - 2).exists:
                            pe.wait_ge(copied[at - 2], copied.done(at - 2))
                        pe.sem_inc(pe_passed, 1)
                        for q in range(ROWS // 2):
                            last = nc.tensor.transpose(own_t[at.h][:, q * P:(q + 1) * P],
                                                       own[:, at.k, 2 * q:2 * q + 2, :].rearrange("p j d -> p (j d)"), ident[:, :])
                        last.then_inc(turned[at], 1)

                    def project(at):
                        pe.wait_ge(copied[at], copied.done(at))
                        if (at - 2).exists:
                            pe.wait_ge(summed[at - 2], summed.done(at - 2))
                        for q in range(ROWS // 2):
                            last = nc.tensor.matmul(out_t[at.h][:, 2 * q:2 * q + 2, :].rearrange("p j d -> p (j d)"),
                                                    own_s[:, at.h, q * P:(q + 1) * P], res_w[:, :], start=True, stop=True)
                        last.then_inc(projected[at], 1)
                    over_blocks(pe, (turn, 0), (project, 1))

                @block.scalar
                def _(act):
                    def copy(at):
                        act.wait_ge(turned[at], turned.done(at))
                        if (at - 2).exists:
                            act.wait_ge(projected[at - 2], projected.done(at - 2))
                        nc.scalar.activation(own_s[:, at.h, :], own_t[at.h][:, :], ACT.Copy).then_inc(copied[at], 1)

                    def squares(at):
                        norm.squares(act, at)

                    def deviations(at):
                        norm.deviations(act, at)
                    over_blocks(act, (deviations, 5), (squares, 4), (copy, 0))

                @block.vector
                def _(dve):
                    def sum_up(at):
                        dve.wait_ge(with_bias[at], with_bias.done(at))
                        dve.wait_ge(projected[at], projected.done(at))
                        if (at - 2).exists:
                            dve.wait_ge(norm.shifted[at - 2], norm.shifted.done(at - 2))
                        nc.vector.tensor_tensor(total[:, at.h], out_t[at.h][:, :, :], biased[:, at.k], ALU.add).then_inc(summed[at], 1)

                    def add_up(at):
                        dve.wait_ge(summed[at], summed.done(at))
                        norm.add_up(dve, at, total[:, at.h])

                    def centre(at):
                        norm.centre(dve, at, total[:, at.h])

                    def invert(at):
                        norm.invert(dve, at)

                    def scale_rows(at):
                        norm.scale_rows(dve, at, stored)
                    over_blocks(dve, (invert, 5), (add_up, 3), (scale_rows, 5), (sum_up, 2), (centre, 3))
            sig.end_phase()

    def relation_norm_phase():
        with ExitStack() as c:
            agg = sb(c, "n3_agg", [P, DEEP, ROWS, D])
            own = sb(c, "n3_own", [P, DEEP, ROWS, D])
            mixed = sb(c, "n3_mixed", [P, 2, ROWS, P])
            mixed_s = sb(c, "n3_mixed_s", [P, 2, ROWS, P])
            slight = sb(c, "n3_slight", [P, 2, ROWS, P])
            leaky = sb(c, "n3_leaky", [P, 2, ROWS, P])
            both = sb(c, "n3_both", [P, 2, ROWS, D])
            total = sb(c, "n3_total", [P, 2, ROWS, D])
            mixed_t = [pb(c, f"n3_mixed_t{h}", [P, ROWS, P]) for h in range(2)]
            out_t = [pb(c, f"n3_out_t{h}", [P, ROWS, P]) for h in range(2)]
            loaded, stored = sig.landing("nodes_loaded", 32), sig.landing("nodes_stored", 16)
            added, summed, united = sig.get("node_added"), sig.get("node_summed"), sig.get("node_united")
            turned, copied, projected = sig.get("rows_turned"), sig.get("rows_copied"), sig.get("projected")
            slighted, leaked, multiplied = sig.get("activated"), sig.get("node_result"), sig.get("node_biased")
            norm = Norm(c, scalar_sums=True)
            with nc.Block() as block:
                @block.sync
                def _(sp):
                    def load(at):
                        if (at - DEEP).exists:
                            sp.wait_ge(multiplied[at - DEEP], multiplied.done(at - DEEP))
                        load_nodes(sp, at, [(sums, agg[:, at.k])], loaded)
                        if (at - DEEP).exists:
                            sp.wait_ge(summed[at - DEEP], summed.done(at - DEEP))
                        load_nodes(sp, at, [(x2_table, own[:, at.k])], loaded)

                    def store(at):
                        store_nodes(sp, at, x3_table, norm.out[:, at.k], norm.ready, stored)
                    over_blocks(sp, (load, 0), (store, 8))
                    wait_stored(sp, stored)

                @block.gpsimd
                def _(pool):
                    def mix(at):
                        pool.wait_ge(loaded[at], loaded.done(at))
                        if (at - 2).exists:
                            pool.wait_ge(turned[at - 2], turned.done(at - 2))
                        nc.gpsimd.tensor_tensor(mixed[:, at.h, :, 0:D], agg[:, at.k], own[:, at.k], ALU.add).then_inc(added[at], 1)
                        nc.gpsimd.tensor_tensor(mixed[:, at.h, :, D:P], agg[:, at.k], own[:, at.k], ALU.mult).then_inc(multiplied[at], 1)
                    over_blocks(pool, (mix, 0))

                @block.tensor
                def _(pe):
                    def turn(at):
                        pe.wait_ge(added[at], added.done(at))
                        pe.wait_ge(multiplied[at], multiplied.done(at))
                        if (at - 2).exists:
                            pe.wait_ge(copied[at - 2], copied.done(at - 2))
                        pe.sem_inc(pe_passed, 1)
                        for j in range(ROWS):
                            last = nc.tensor.transpose(mixed_t[at.h][:, j, :], mixed[:, at.h, j, :], ident[:, :])
                        last.then_inc(turned[at], 1)

                    def write(at):
                        pe.wait_ge(copied[at], copied.done(at))
                        if (at - 2).exists:
                            pe.wait_ge(slighted[at - 2], slighted.done(at - 2))
                            pe.wait_ge(leaked[at - 2], leaked.done(at - 2))
                        for j in range(ROWS):
                            last = nc.tensor.matmul(out_t[at.h][:, j, :], mixed_s[:, at.h, j, :], fc2[:, :], start=True, stop=True)
                        last.then_inc(projected[at], 1)
                    over_blocks(pe, (turn, 0), (write, 1))

                @block.scalar
                def _(act):
                    def copy(at):
                        act.wait_ge(turned[at], turned.done(at))
                        if (at - 2).exists:
                            act.wait_ge(projected[at - 2], projected.done(at - 2))
                        nc.scalar.activation(mixed_s[:, at.h], mixed_t[at.h][:, :, :], ACT.Copy).then_inc(copied[at], 1)

                    def slight_of(at):
                        act.wait_ge(projected[at], projected.done(at))
                        if (at - 2).exists:
                            act.wait_ge(leaked[at - 2], leaked.done(at - 2))
                        nc.scalar.activation(slight[:, at.h], out_t[at.h][:, :, :], ACT.Copy, scale=0.01).then_inc(slighted[at], 1)

                    def squares(at):
                        norm.squares(act, at)

                    def deviations(at):
                        norm.deviations(act, at)
                    over_blocks(act, (deviations, 5), (squares, 4), (copy, 0), (slight_of, 1))

                @block.vector
                def _(dve):
                    def bend(at):
                        dve.wait_ge(slighted[at], slighted.done(at))
                        if (at - 2).exists:
                            dve.wait_ge(united[at - 2], united.done(at - 2))
                        nc.vector.tensor_tensor(leaky[:, at.h], out_t[at.h][:, :, :], slight[:, at.h], ALU.max).then_inc(leaked[at], 1)

                    def unite(at):
                        dve.wait_ge(leaked[at], leaked.done(at))
                        if (at - 2).exists:
                            dve.wait_ge(summed[at - 2], summed.done(at - 2))
                        nc.vector.tensor_tensor(both[:, at.h], leaky[:, at.h, :, 0:D], leaky[:, at.h, :, D:P], ALU.add).then_inc(united[at], 1)

                    def sum_up(at):
                        dve.wait_ge(united[at], united.done(at))
                        dve.wait_ge(loaded[at], loaded.done(at))
                        if (at - 2).exists:
                            dve.wait_ge(norm.shifted[at - 2], norm.shifted.done(at - 2))
                        nc.vector.tensor_tensor(total[:, at.h], both[:, at.h], own[:, at.k], ALU.add).then_inc(summed[at], 1)

                    def add_up(at):
                        dve.wait_ge(summed[at], summed.done(at))
                        norm.add_up(dve, at, total[:, at.h])

                    def centre(at):
                        norm.centre(dve, at, total[:, at.h])

                    def invert(at):
                        norm.invert(dve, at)

                    def scale_rows(at):
                        norm.scale_rows(dve, at, stored)
                    over_blocks(dve, (bend, 2), (add_up, 3), (unite, 2), (invert, 5), (sum_up, 2), (centre, 3), (scale_rows, 5))
            sig.end_phase()

    def update_norm_phase():
        with ExitStack() as c:
            pair = sb(c, "n4_pair", [P, DEEP, ROWS, P])
            pair_s = sb(c, "n4_pair_s", [P, 2, ROWS * P])
            hidden = sb(c, "n4_hidden", [HID, 2, ROWS * P])
            biased = sb(c, "n4_biased", [P, DEEP, ROWS, D])
            total = sb(c, "n4_total", [P, 2, ROWS, D])
            pair_t = [pb(c, f"n4_pair_t{k}", [P, 512]) for k in range(2)]
            hidden_t = [pb(c, f"n4_hidden_t{h}", [HID, 1024]) for h in range(2)]
            out_t = [pb(c, f"n4_out_t{h}", [P, ROWS, D]) for h in range(2)]
            loaded, stored = sig.landing("nodes_loaded", 32), sig.landing("nodes_stored", 16)
            summed, with_bias = sig.get("node_summed"), sig.get("node_biased")
            turned, copied, projected = sig.get("rows_turned", 2), sig.get("rows_copied", 2), sig.get("projected")
            activated, written = sig.get("activated"), sig.get("scored")
            norm = Norm(c)
            with nc.Block() as block:
                @block.sync
                def _(sp):
                    def load(at):
                        if (at - DEEP).exists:
                            sp.wait_ge(turned[at - DEEP], turned.done(at - DEEP))
                            sp.sem_inc(sp_passed, 1)
                            sp.wait_ge(with_bias[at - DEEP], with_bias.done(at - DEEP))
                        load_nodes(sp, at, [(x3_table, pair[:, at.k, :, 0:D]), (sums, pair[:, at.k, :, D:P])], loaded)

                    def store(at):
                        store_nodes(sp, at, out, norm.out[:, at.k], norm.ready, stored)
                    over_blocks(sp, (load, 0), (store, 8))
                    wait_stored(sp, stored)

                @block.gpsimd
                def _(pool):
                    def add(at):
                        pool.wait_ge(loaded[at], loaded.done(at))
                        if (at - DEEP).exists:
                            pool.wait_ge(summed[at - DEEP], summed.done(at - DEEP))
                        nc.gpsimd.tensor_tensor(biased[:, at.k], pair[:, at.k, :, 0:D], over_rows(u_b2), ALU.add).then_inc(with_bias[at], 1)
                    over_blocks(pool, (add, 0))

                @block.tensor
                def _(pe):
                    def turn(at):
                        pe.wait_ge(loaded[at], loaded.done(at))
                        for k in range(2):
                            if (at - 1).exists:
                                pe.wait_ge(copied[at - 1], copied.part(at - 1, k + 1))
                            pe.sem_inc(pe_passed, 1)
                            for j in range(4):
                                last = nc.tensor.transpose(pair_t[k][:, j * P:(j + 1) * P], pair[:, at.k, 4 * k + j, :], ident[:, :])
                            last.then_inc(turned[at], 1)

                    def hide(at):
                        pe.wait_ge(copied[at], copied.done(at))
                        if (at - 2).exists:
                            pe.wait_ge(activated[at - 2], activated.done(at - 2))
                        for k in range(2):
                            last = nc.tensor.matmul(hidden_t[at.h][:, k * 512:(k + 1) * 512], u_w1[:, :],
                                                    pair_s[:, at.h, k * 512:(k + 1) * 512], start=True, stop=True)
                        last.then_inc(projected[at], 1)

                    def write(at):
                        pe.wait_ge(activated[at], activated.done(at))
                        if (at - 2).exists:
                            pe.wait_ge(summed[at - 2], summed.done(at - 2))
                        for j in range(ROWS):
                            last = nc.tensor.matmul(out_t[at.h][:, j, :], hidden[:, at.h, j * P:(j + 1) * P], u_w2[:, :],
                                                    start=True, stop=True)
                        last.then_inc(written[at], 1)
                    over_blocks(pe, (turn, 0), (hide, 1), (write, 2))

                @block.scalar
                def _(act):
                    def copy(at):
                        if (at - 2).exists:
                            act.wait_ge(projected[at - 2], projected.done(at - 2))
                        for k in range(2):
                            act.wait_ge(turned[at], turned.part(at, k + 1))
                            nc.scalar.activation(pair_s[:, at.h, k * 512:(k + 1) * 512], pair_t[k][:, :], ACT.Copy).then_inc(copied[at], 1)

                    def rectify(at):
                        act.wait_ge(projected[at], projected.done(at))
                        if (at - 2).exists:
                            act.wait_ge(written[at - 2], written.done(at - 2))
                        nc.scalar.activation(hidden[:, at.h, :], hidden_t[at.h][:, :], ACT.Relu, bias=u_b1[:, 0:1]).then_inc(activated[at], 1)

                    def squares(at):
                        norm.squares(act, at)

                    def deviations(at):
                        norm.deviations(act, at)
                    over_blocks(act, (deviations, 5), (squares, 4), (copy, 0), (rectify, 1))

                @block.vector
                def _(dve):
                    def start(at):
                        dve.wait_ge(with_bias[at], with_bias.done(at))
                        dve.wait_ge(written[at], written.done(at))
                        if (at - 2).exists:
                            dve.wait_ge(norm.shifted[at - 2], norm.shifted.done(at - 2))
                        nc.vector.tensor_tensor(total[:, at.h], out_t[at.h][:, :, :], biased[:, at.k], ALU.add).then_inc(summed[at], 1)
                        dve.wait_ge(summed[at], summed.done(at))
                        norm.add_up(dve, at, total[:, at.h])

                    def centre(at):
                        norm.centre(dve, at, total[:, at.h])

                    def power(at):
                        norm.power_of(dve, at)

                    def invert(at):
                        norm.invert(dve, at)

                    def scale_rows(at):
                        norm.scale_rows(dve, at, stored)
                    over_blocks(dve, (invert, 5), (power, 4), (scale_rows, 5), (start, 3), (centre, 3))
            sig.end_phase()

    scale_phase()
    sum_phase(y_table)
    gcn_phase()
    sum_phase(h_table)
    first_norm_phase()
    attention_phase(x1_table, relations=False)
    attention_norm_phase()
    attention_phase(x2_table, relations=True)
    relation_norm_phase()
    message_phase(x3_table)
    update_norm_phase()


_INS = ["x", "src", "dst", "edge_attr_32", "edge_attr_64", "edge_type_10", "L0_gnn_W1", "L0_gnn_b1", "L0_gnn_W2",
        "L0_gnn_b2", "L1_gnn_W_out", "L1_gnn_b_out", "L1_gnn_attn_w", "L1_gnn_res_W", "L1_gnn_res_b",
        "L2_gnn_relation_weight", "L2_gnn_res_fc_w", "L2_gnn_res_fc2_w", "L3_gnn_mW1", "L3_gnn_mb1", "L3_gnn_mW2",
        "L3_gnn_mb2", "L3_gnn_uW1", "L3_gnn_ub1", "L3_gnn_uW2", "L3_gnn_ub2"]


def kernel(**inputs):
    import numpy as _np
    import concourse.bacc as _bacc
    from concourse import mybir as _mybir
    from concourse.bass_utils import run_bass_kernel_spmd as _run

    nc = _bacc.Bacc("TRN2", target_bir_lowering=False, num_devices=1)
    arrays, args = {}, {}
    for name in _INS:
        a = _np.ascontiguousarray(inputs[name])
        arrays[f"in_{name}_dram"] = a
        args[name] = nc.dram_tensor(f"in_{name}_dram", a.shape, _mybir.dt.from_np(a.dtype), kind="ExternalInput").ap()
    out = nc.dram_tensor("out_dram", (NODES, D), F32, kind="ExternalOutput").ap()
    bass_gnn(nc, args, out)
    r = _run(nc, [arrays], core_ids=[0])
    return r.results[0]["out_dram"]
```
